# Optimizing a Trainium2 kernel written in Bass

```python
import numpy as np
import jax
import jax.numpy as jnp

def _softmax(x, axis=-1):
    return jax.nn.softmax(x, axis=axis)

def _gelu(x):
    return jax.nn.gelu(x, approximate=True)

def _silu(x):
    return jax.nn.silu(x)

def _sigmoid(x):
    return jax.nn.sigmoid(x)

def _layernorm(x, axis=-1, eps=1e-05):
    m = jnp.mean(x, axis=axis, keepdims=True)
    v = jnp.var(x, axis=axis, keepdims=True)
    return (x - m) / jnp.sqrt(v + eps)

def _scatter_add(tgt, idx, src, axis=0):
    return tgt.at[idx].add(src)

def _segment_sum(src, seg, n):
    return jax.ops.segment_sum(src, seg, n)
kernel_name = 'mk_flamingo_gated_d1_seqx_r2_4c112f'

def setup_inputs(seed: int=0):
    np.random.seed(seed)
    _w = jnp.asarray

    def _rec_inputs():
        import jax
        import jax.numpy as jnp
        _rk = jax.random.key(seed)
        x = -0.0002928 + 1 * jax.random.normal(jax.random.fold_in(_rk, 1), (8, 224, 512), jnp.float32)
        _lenS = 224 - jax.random.randint(jax.random.fold_in(_rk, 7), (8,), 0, max(1, 224 // 4) + 1, jnp.int32)
        _lenS2 = 750 - jax.random.randint(jax.random.fold_in(_rk, 8), (8,), 0, max(1, 750 // 4) + 1, jnp.int32)
        _ctx_1024P = jax.random.normal(jax.random.fold_in(_rk, 11), (8, 16, 512), jnp.float32)
        _ctx_1024c = jax.random.dirichlet(jax.random.fold_in(_rk, 511), 0.3 * jnp.ones((16,), jnp.float32), (8, 750))
        _ctx_1024t = jnp.einsum('bsk,bkd->bsd', _ctx_1024c, _ctx_1024P)
        _ctx_1024t = _ctx_1024t * jax.lax.rsqrt(jnp.mean(jnp.square(_ctx_1024t)) + 1e-12) * 0.953939
        ctx_1024 = -1.39393e-06 + 0.999914 * (_ctx_1024t + 0.3 * jax.random.normal(jax.random.fold_in(_rk, 611), (8, 750, 512), jnp.float32))
        _g = jax.random.normal(jax.random.fold_in(_rk, 9001), (2, 1), jnp.float32)
        _g = jnp.sign(_g) * jnp.maximum(jnp.abs(_g), 1.0) + (_g == 0) * 1.0
        g_xattn = _g[0]
        g_ffn = _g[1]
        return (x, ctx_1024, g_xattn, g_ffn)
    x, ctx_1024, g_xattn, g_ffn = _rec_inputs()

    def _L0_xattn_setup():
        import jax, jax.numpy as jnp
        import numpy as np
        QUERY_DIM = 512
        CONTEXT_DIM = 512
        HEADS = 8
        DIM_HEAD = 64
        INNER = HEADS * DIM_HEAD
        SCALE = DIM_HEAD ** (-0.5)
        key = jax.random.key(seed)
        ks = jax.random.split(key, 7)
        B, N, M = (2, 1024, 1024)
        x = jax.random.normal(ks[0], (B, N, QUERY_DIM), dtype=jnp.float32)
        context = jax.random.normal(ks[1], (B, M, CONTEXT_DIM), dtype=jnp.float32)
        Wq = jax.random.normal(ks[2], (QUERY_DIM, INNER), dtype=jnp.float32) * QUERY_DIM ** (-0.5)
        Wk = jax.random.normal(ks[3], (CONTEXT_DIM, INNER), dtype=jnp.float32) * CONTEXT_DIM ** (-0.5)
        Wv = jax.random.normal(ks[4], (CONTEXT_DIM, INNER), dtype=jnp.float32) * CONTEXT_DIM ** (-0.5)
        Wo = jax.random.normal(ks[5], (INNER, QUERY_DIM), dtype=jnp.float32) * INNER ** (-0.5)
        bo = jax.random.normal(ks[6], (QUERY_DIM,), dtype=jnp.float32) * 0.01
        return {'x': x, 'context': context, 'Wq': Wq, 'Wk': Wk, 'Wv': Wv, 'Wo': Wo, 'bo': bo}
    _L0_xattn_all = _L0_xattn_setup()
    _L0_xattn_in = {k: v for k, v in _L0_xattn_all.items() if k in ('Wq', 'Wk', 'Wv', 'Wo', 'bo')}
    del _L0_xattn_all

    def _L0_ffn_setup():
        import jax, jax.numpy as jnp
        import numpy as np
        TEMPERATURE = 0.5
        CAPACITY_FACTOR = 1.25
        TOP_K = 1
        key = jax.random.key(seed)
        ks = jax.random.split(key, 5)
        B, S, D, H, E = (4, 1024, 512, 1024, 8)
        s = 0.02
        return {'x': jax.random.normal(ks[0], (B, S, D), jnp.float32), 'gate_w': jax.random.normal(ks[1], (E, D), jnp.float32) * s, 'gate_b': jnp.zeros((E,), jnp.float32), 'rms_w': jnp.ones((E,), jnp.float32), 'w1': jax.random.normal(ks[2], (E, D, H), jnp.float32) * s, 'b1': jnp.zeros((E, H), jnp.float32), 'w2': jax.random.normal(ks[3], (E, H, D), jnp.float32) * s, 'b2': jnp.zeros((E, D), jnp.float32)}
    _L0_ffn_all = _L0_ffn_setup()
    _L0_ffn_in = {k: v for k, v in _L0_ffn_all.items() if k in ('gate_w', 'gate_b', 'rms_w', 'w1', 'b1', 'w2', 'b2')}
    del _L0_ffn_all
    return {'x': x, 'ctx_1024': ctx_1024, 'g_xattn': g_xattn, 'g_ffn': g_ffn, 'L0_xattn_Wq': _L0_xattn_in['Wq'], 'L0_xattn_Wk': _L0_xattn_in['Wk'], 'L0_xattn_Wv': _L0_xattn_in['Wv'], 'L0_xattn_Wo': _L0_xattn_in['Wo'], 'L0_xattn_bo': _L0_xattn_in['bo'], 'L0_ffn_gate_w': _L0_ffn_in['gate_w'], 'L0_ffn_gate_b': _L0_ffn_in['gate_b'], 'L0_ffn_rms_w': _L0_ffn_in['rms_w'], 'L0_ffn_w1': _L0_ffn_in['w1'], 'L0_ffn_b1': _L0_ffn_in['b1'], 'L0_ffn_w2': _L0_ffn_in['w2'], 'L0_ffn_b2': _L0_ffn_in['b2']}

def reference(x, ctx_1024, g_xattn, g_ffn, L0_xattn_Wq, L0_xattn_Wk, L0_xattn_Wv, L0_xattn_Wo, L0_xattn_bo, L0_ffn_gate_w, L0_ffn_gate_b, L0_ffn_rms_w, L0_ffn_w1, L0_ffn_b1, L0_ffn_w2, L0_ffn_b2):
    import jax
    import jax.numpy as jnp

    def _L0_xattn_ref(x, context, Wq, Wk, Wv, Wo, bo):
        import jax, jax.numpy as jnp
        import numpy as np
        QUERY_DIM = 512
        CONTEXT_DIM = 512
        HEADS = 8
        DIM_HEAD = 64
        INNER = HEADS * DIM_HEAD
        SCALE = DIM_HEAD ** (-0.5)
        B, N, _ = x.shape
        M = context.shape[1]
        q = (x @ Wq).reshape(B, N, HEADS, DIM_HEAD)
        k = (context @ Wk).reshape(B, M, HEADS, DIM_HEAD)
        v = (context @ Wv).reshape(B, M, HEADS, DIM_HEAD)
        sim = jnp.einsum('bihd,bjhd->bhij', q.astype(jnp.float32), k.astype(jnp.float32)) * SCALE
        attn = jax.nn.softmax(sim, axis=-1).astype(v.dtype)
        out = jnp.einsum('bhij,bjhd->bihd', attn, v).reshape(B, N, INNER)
        return out @ Wo + bo

    def _L0_ffn_ref(x, gate_w, gate_b, rms_w, w1, b1, w2, b2):
        import jax, jax.numpy as jnp
        import numpy as np
        TEMPERATURE = 0.5
        CAPACITY_FACTOR = 1.25
        TOP_K = 1
        B, S, D = x.shape
        E = gate_w.shape[0]
        xf = x.reshape(-1, D)
        N = xf.shape[0]
        logits = xf @ gate_w.T + gate_b
        eps = jnp.finfo(logits.dtype).eps
        ms = jnp.mean(logits * logits, axis=-1, keepdims=True)
        logits = logits * jax.lax.rsqrt(ms + eps) * rms_w
        gates = jax.nn.softmax(logits / TEMPERATURE, axis=-1)
        g, idx = jax.lax.top_k(gates, TOP_K)
        g, idx = (g[:, 0], idx[:, 0])
        capacity = min(int(np.ceil(N * TOP_K / E * CAPACITY_FACTOR)), N)
        counts = jnp.zeros((E,), jnp.int32).at[idx].add(1)
        active = (counts > 0) & (capacity >= 1)
        mask = active[idx].astype(gates.dtype)
        masked = g * mask
        norm_g = masked / (masked + 1e-06)
        h = jax.nn.gelu(jnp.einsum('nd,edh->neh', xf, w1) + b1, approximate=False)
        y = jnp.einsum('neh,ehd->ned', h, w2) + b2
        out = (y * norm_g[:, None, None]).sum(axis=1)
        return out.reshape(B, S, D)
    x = x + jnp.tanh(g_xattn[0]) * _L0_xattn_ref(_layernorm(x, axis=-1), ctx_1024, L0_xattn_Wq, L0_xattn_Wk, L0_xattn_Wv, L0_xattn_Wo, L0_xattn_bo)
    x = x + jnp.tanh(g_ffn[0]) * _L0_ffn_ref(_layernorm(x, axis=-1), L0_ffn_gate_w, L0_ffn_gate_b, L0_ffn_rms_w, L0_ffn_w1, L0_ffn_b1, L0_ffn_w2, L0_ffn_b2)
    return x

_drawn_inputs = setup_inputs


def setup_inputs(seed=0):
    import zlib

    import numpy as np

    out = dict(_drawn_inputs(seed))
    spreads = {'L0_ffn_gate_b': (0.0, 0.8),
     'L0_ffn_rms_w': (1.0, 0.6),
     'L0_ffn_b1': (0.0, 0.1),
     'L0_ffn_b2': (0.0, 0.1)}
    factors = {'L0_xattn_bo': 8.0, 'L0_ffn_gate_w': 8.0}
    for name, (base, spread) in spreads.items():
        noise = np.random.default_rng([zlib.crc32(name.encode()), seed]).standard_normal(out[name].shape)
        drawn = base * np.exp(spread * noise) if base else spread * noise
        out[name] = jnp.asarray(drawn.astype(out[name].dtype))
    for name, factor in factors.items():
        out[name] = (out[name] * factor).astype(out[name].dtype)
    return out
```

```python
from contextlib import ExitStack

import concourse.bass as bass
from concourse import mybir

ALU = mybir.AluOpType
ACT = mybir.ActivationFunctionType
F32 = mybir.dt.float32
F32R = mybir.dt.float32r
AX = mybir.AxisListType

P = 128
B, NQ, D = 8, 224, 512
NK = 750
H, DH = 8, 64
G = 4
KC = D // P
QT = NQ // 2
KT = NK // 6
NKT = NK // KT
SK = NK // 3
HALVES = [(0, 376), (376, NK)]
N = B * NQ
NE, HID = 8, 1024
HT = HID // P
TT = N // P
CHUNKS = [(0, 4), (4, 4), (8, 3), (11, 3)]
LN_EPS = 1e-5
RMS_EPS = 1.1920928955078125e-07
TEMPERATURE = 0.5
NORM_EPS = 1e-6


def number(item, b):
    kind, db = item[0], item[1]
    n = b + db
    if kind == "C":
        return n * NKT + (item[2] + 1)
    if kind in ("X", "O", "Y"):
        return n * 2 + (item[2] + 1)
    if kind == "K":
        return n * 8 + (item[2] * 4 + item[3] * 2 + item[4] + 1)
    if kind == "Q":
        return n * 4 + (item[2] * 2 + item[3] + 1)
    if kind == "V":
        return n * 12 + (item[2] * 6 + item[3] + 1)
    if kind == "T":
        return n * 24 + (item[2] * 3 + item[3] + 1)
    if kind == "S" or kind == "R":
        return n * 16 + (item[2] * 2 + item[3] + 1)
    assert kind == "P"
    return n * 8 + (item[2] + 1)


def pair_number(b, pair):
    return b * 4 + (pair + 1)


BANKED = "CXKQVTOY"

FILL = [
    [[("K", 0, 1, 0, 0)], [("Q", 0, 1, 0)], [("K", 0, 1, 0, 1)], [("O", -1, 0)]],
    [[("O", -1, 1)], [("V", 0, 1, 0)], [("V", 0, 1, 1)], [("V", 0, 1, 2)]],
    [[("Y", -1, 0)], [("V", 0, 1, 3)], [("V", 0, 1, 4)], [("Y", -1, 1)]],
    [[("K", 0, 1, 1, 0)], [("Q", 0, 1, 1)], [("K", 0, 1, 1, 1)], [("V", 0, 1, 5)]],
    [[("C", 1, 0), ("C", 1, 1)], [("C", 1, 2)], [("C", 1, 3)], [("X", 1, 0)]],
    [[("K", 1, 0, 0, 0)], [("C", 1, 4)], [("X", 1, 1)], [("C", 1, 5), ("V", 1, 0, 0)]],
    [[("K", 1, 0, 0, 1)], [("Q", 1, 0, 0)], [("V", 1, 0, 1)], [("V", 1, 0, 2), ("V", 1, 0, 3)]],
    [[("K", 1, 0, 1, 0)], [("K", 1, 0, 1, 1)], [("Q", 1, 0, 1)], [("V", 1, 0, 4), ("V", 1, 0, 5)]],
]


def body_plan(first, last):
    plan = []
    for h in range(H):
        fill = [[i for i in f if not (first and i[1] < 0) and not (last and i[1] > 0)] for f in FILL[h]]
        nxt = (0, h + 1) if h < H - 1 else (1, 0)
        if not (last and nxt[0]):
            plan += [("S", *nxt, 0), ("S", *nxt, 1)]
        plan += fill[0]
        if not (last and nxt[0]):
            plan += [("R", *nxt, 0)]
        plan += [("T", 0, h, 0)] + fill[1]
        if not (last and nxt[0]):
            plan += [("R", *nxt, 1)]
        plan += [("T", 0, h, 1)] + fill[2] + [("T", 0, h, 2)] + fill[3] + [("P", 0, h)]
        plan += [("END", 0, h)]
    return plan


HEAD_PLAN = ([("C", 0, t) for t in range(3)] + [("X", 0, 0)] + [("C", 0, t) for t in range(3, 6)] + [("X", 0, 1)]
             + [("K", 0, 0, 0, 0), ("K", 0, 0, 0, 1), ("Q", 0, 0, 0), ("S", 0, 0, 0), ("S", 0, 0, 1),
                ("K", 0, 0, 1, 0), ("R", 0, 0, 0), ("K", 0, 0, 1, 1), ("R", 0, 0, 1), ("Q", 0, 0, 1)]
             + [("V", 0, 0, t) for t in range(6)])
TAIL_PLAN = [("O", 0, 0), ("O", 0, 1), ("Y", 0, 0), ("Y", 0, 1)]


def banks(plan, before):
    def in_turn(items):
        items = [i for i in items if i[0] in BANKED]
        return [((n - len(items)) % 3, i) for n, i in enumerate(items)]

    last = {bank: item for bank, item in in_turn(before)}
    out = {}
    for bank, item in in_turn(plan):
        out[item] = (bank, last.get(bank))
        last[bank] = item
    return out


def shifted(plan, d):
    return [(i[0], i[1] + d, *i[2:]) for i in plan]


def alone(eng, waits_passed):
    eng.sem_inc(waits_passed, 1)


def flamingo_kernel(nc, x, ctx, g_xattn, g_ffn, Wq, Wk, Wv, Wo, bo, gate_w, gate_b, rms_w, w1, b1, w2, b2, out,
                    x2_scratch, xt_scratch):
    FIRST, MIDDLE, LAST = body_plan(True, False), body_plan(False, False), body_plan(False, True)
    bank_of = {
        "head": banks(HEAD_PLAN, []),
        "first": banks(FIRST, HEAD_PLAN),
        "middle": banks(MIDDLE, shifted(MIDDLE, -1)),
        "last": banks(LAST, shifted(MIDDLE, -1)),
        "tail": banks(TAIL_PLAN, LAST),
    }

    x_rows = x.rearrange("b q d -> (b q) d")
    out_rows = out.rearrange("b q d -> (b q) d")

    with ExitStack() as st:
        def sem(name):
            return st.enter_context(nc.semaphore(name))

        def alloc(stack, name, shape, dt=F32):
            return stack.enter_context(nc.sbuf_tensor(name, shape, dt))

        ident = alloc(st, "ident", [P, P])
        tanh_g = alloc(st, "tanh_g", [P, 2])
        minus_half = alloc(st, "minus_half", [P, 16])
        ps = [st.enter_context(nc.psum_tensor(f"bank{i}", [P, 512], F32)) for i in range(3)]
        ps_scores = [st.enter_context(nc.psum_tensor(f"scores{i}", [P, 4, 256], F32)) for i in range(2)]
        ps_pv = st.enter_context(nc.psum_tensor("pv_bank", [P, 512], F32))

        with ExitStack() as att:
            def a(name, shape, dt=F32):
                return alloc(att, name, shape, dt)

            wk = a("wk", [P, 2, KC, D], F32R)
            wv = a("wv", [P, 2, KC, D], F32R)
            ctxT = a("ctxT", [P, 2, KC, NK], F32R)
            wq = a("wq", [P, 2, KC, D], F32R)
            kst, vst, qst = [None] * 2, [None] * 2, [None] * 2
            kst[0] = a("keys0", [P, G, NK], F32R)
            vst[0] = a("values0", [P, NKT, G // 2, 4, DH], F32R)
            qst[0] = a("queries0", [P, 2, G, NQ], F32R)
            ctx_raw = a("ctx_raw", [P, 2, D])
            kst[1] = a("keys1", [P, G, NK], F32R)
            vst[1] = a("values1", [P, NKT, G // 2, 4, DH], F32R)
            qst[1] = a("queries1", [P, 2, G, NQ], F32R)
            wo = a("wo", [P, 2, KC, D], F32R)
            xnT = a("xnT", [P, 2, KC, NQ], F32R)
            xa = a("xa", [P, 2, D])
            stats = a("stats", [P, 4, 6])
            mean_var = a("mean_var", [P, 4, 2])
            rstd = a("rstd", [P, 4])
            neg_max = a("neg_max", [P, 4])
            row_sum = a("row_sum", [P, 4])
            row_inv = a("row_inv", [P, 4])
            bo_t = a("bo_t", [P, D])
            with ExitStack() as staging:
                w_raw = alloc(staging, "w_raw", [P, 4, KC, D])
            probs = a("probs", [P, 4, NK])
            probsT = a("probsT", [P, 2, 3, 2 * NQ], F32R)
            att_tmp = a("att_tmp", [P, NQ])
            att_sum = a("att_sum", [P, NQ])
            attT = a("attT", [P, 2, H // 2, NQ], F32R)
            xres = a("xres", [P, 2, D])
            yT = a("yT", [P, 2, KC, QT], F32R)

        ffn = st
        xT = alloc(ffn, "xT", [P, 2, KC, N], F32R)
        w_stage = alloc(ffn, "w_stage", [P, 2, HID])
        w1s = alloc(ffn, "w1s", [P, 2, KC, HID], F32R)
        hs = alloc(ffn, "hs", [P, 2, HT, 512], F32R)
        w2s = alloc(ffn, "w2s", [P, 2, HT, D], F32R)
        acc = alloc(ffn, "acc", [P, TT, D])
        h_full = alloc(ffn, "h_full", [P, 2, 512])
        x2_tile = alloc(ffn, "x2_tile", [P, 2, D])
        b1T = alloc(ffn, "b1T", [P, NE * HT])
        gate_st = alloc(ffn, "gate_st", [P, KC, P], F32R)
        logits = alloc(ffn, "logits", [P, TT, NE])
        gate_small = alloc(ffn, "gate_small", [P, 6, TT])
        token_gate = alloc(ffn, "token_gate", [P, TT])
        b1_rows = x2_tile[0:NE * HT, 0, 0:P]
        gate_rows = x2_tile[0:NE, 1, :]
        b2_rows = h_full[0:NE, 0, :]
        ones8 = h_full[0:NE, 1, 0:P]
        gate_lo = gate_small
        scaleb = alloc(ffn, "scaleb", [P, 2, NE])
        lg_lo = alloc(ffn, "lg_lo", [P, TT, NE])

        in_psum = {k: sem(f"{k}_in_psum") for k in "CXKQVTOYSP"}
        hi_out = {k: sem(f"{k}_hi_out") for k in "CXKQVTY"}
        lo_out = {k: sem(f"{k}_lo_out") for k in "CXKQVTOY"}
        consts_set = sem("consts_set")
        g_loaded, tanh_done = sem("g_loaded"), sem("tanh_done")
        bo_loaded, bo_scaled = sem("bo_loaded"), sem("bo_scaled")
        w_loaded = [sem(f"w_loaded{i}") for i in range(4)]
        w_hi, w_lo = sem("w_hi"), sem("w_lo")
        ctx_loaded = [sem(f"ctx_loaded{i}") for i in range(2)]
        x_loaded = [sem(f"x_loaded{i}") for i in range(2)]
        xres_loaded = [sem(f"xres_loaded{i}") for i in range(2)]
        ln_step, ln_var, ln_rstd, ln_out = sem("ln_step"), sem("ln_var"), sem("ln_rstd"), sem("ln_out")
        xres_biased = sem("xres_biased")
        max_out, exp_out, inv_out, probs_scaled = sem("max_out"), sem("exp_out"), sem("inv_out"), sem("probs_scaled")
        pv_swapped, pv_summed, att_hi, att_lo = sem("pv_swapped"), sem("pv_summed"), sem("att_hi"), sem("att_lo")
        x2_stored = [sem(f"x2_stored{i}") for i in range(2)]
        yT_stored = sem("yT_stored")

        xT_loaded = [sem(f"xT_loaded{i}") for i in range(len(CHUNKS))]
        small_loaded, small_psum, small_out = sem("small_loaded"), sem("small_psum"), sem("small_out")
        scale_loaded = sem("scale_loaded")
        stage_loaded = [sem(f"stage_loaded{i}") for i in range(2)]
        piece_hi, piece_split = sem("piece_hi"), sem("piece_split")
        acc_set = sem("acc_set")
        h_psum, h_act, h_split = sem("h_psum"), sem("h_act"), sem("h_split")
        y_psum, y_added = sem("y_psum"), sem("y_added")
        gate_psum, gate_copied, gate_tr, gate_step = sem("gate_psum"), sem("gate_copied"), sem("gate_tr"), sem("gate_step")
        gate_pow, gate_exp = sem("gate_pow"), sem("gate_exp")
        x2_loaded = [sem(f"x2_loaded{i}") for i in range(2)]
        final_step, out_ready = sem("final_step"), sem("out_ready")
        out_stored = [sem(f"out_stored{i}") for i in range(2)]

        passed = {k: sem(f"{k}_waits_passed") for k in ("sp", "act", "dve", "pool")}

        block = st.enter_context(nc.Block())

        def batches(eng, run):
            run("first", FIRST, 0)
            with eng.Fori(1, B - 1) as b:
                run("middle", MIDDLE, b)
            run("last", LAST, B - 1)

        @block.sync
        def _(sp):
            def load_ctx(b, t):
                if isinstance(b, int) and b == 0:
                    if t >= 2:
                        sp.wait_ge(in_psum["C"], t - 1)
                else:
                    sp.wait_ge(in_psum["C"], b * NKT + (t - 1))
                    alone(sp, passed["sp"])
                sp.dma_start(ctx_raw[0:KT, t % 2, :], ctx[b, t * KT:(t + 1) * KT, :]).then_inc(ctx_loaded[t % 2], 16)

            def load_w(i, w):
                sp.dma_start(w_raw[:, i], w.rearrange("(c p) n -> p c n", p=P)).then_inc(w_loaded[i], 16)

            def load_x(b, qt):
                sp.dma_start(xa[0:QT, qt, :], x[b, qt * QT:(qt + 1) * QT, :]).then_inc(x_loaded[qt], 16)

            def load_xres(b, qt):
                sp.dma_start(xres[0:QT, qt, :], x[b, qt * QT:(qt + 1) * QT, :]).then_inc(xres_loaded[qt], 16)

            def store_x2(b, qt):
                sp.wait_ge(lo_out["O"], number(("O", 0, qt), b))
                alone(sp, passed["sp"])
                sp.dma_start(x2_scratch[b, qt * QT:(qt + 1) * QT, :], xres[0:QT, qt, :]).then_inc(x2_stored[qt], 16)

            def store_yT(b, qt):
                sp.wait_ge(lo_out["Y"], number(("Y", 0, qt), b))
                alone(sp, passed["sp"])
                for part in range(2):
                    sp.dma_start(xt_scratch[part, :, :, b, qt * QT:(qt + 1) * QT],
                                 yT[:, part].bitcast(F32)).then_inc(yT_stored, 16)

            def load_xres_next(b):
                for qt in range(2):
                    sp.wait_ge(x2_stored[qt], b * 16)
                    alone(sp, passed["sp"])
                    sp.wait_ge(ln_out, b * 4 + (qt + 1))
                    alone(sp, passed["sp"])
                    load_xres(b, qt)

            sp.dma_start(tanh_g[:, 0:1], g_xattn.partition_broadcast(P)).then_inc(g_loaded, 16)
            sp.dma_start(tanh_g[:, 1:2], g_ffn.partition_broadcast(P)).then_inc(g_loaded, 16)
            load_ctx(0, 0)
            load_ctx(0, 1)
            load_w(0, Wk)
            for qt in range(2):
                load_x(0, qt)
            for t in range(2, NKT):
                load_ctx(0, t)
            load_w(1, Wq)
            load_w(2, Wv)
            load_w(3, Wo)
            sp.dma_start(bo_t[:, :], bo.partition_broadcast(P)).then_inc(bo_loaded, 16)

            def batch(name, plan, b):
                if name == "first":
                    sp.wait_ge(w_hi, 4)
                    sp.wait_ge(w_lo, 4)
                    for qt in range(2):
                        load_xres(b, qt)
                else:
                    store_x2(b - 1, 0)
                    store_x2(b - 1, 1)
                    load_xres_next(b)
                    store_yT(b - 1, 0)
                    store_yT(b - 1, 1)
                if name != "last":
                    for qt in range(2):
                        if name != "first":
                            sp.wait_ge(in_psum["Y"], number(("Y", -1, qt), b))
                            alone(sp, passed["sp"])
                        sp.wait_ge(in_psum["X"], number(("X", 0, qt), b))
                        alone(sp, passed["sp"])
                        load_x(b + 1, qt)
                    for t in range(NKT):
                        load_ctx(b + 1, t)

            batches(sp, batch)

            def load_piece(e, which, j, n):
                if not (isinstance(n, int) and n < 2):
                    sp.wait_ge(piece_split, n - 1)
                    alone(sp, passed["sp"])
                if which == 1:
                    src = w1[e, j * P:(j + 1) * P, :]
                    dst = w_stage[:, j % 2, :]
                else:
                    src = w2[e, 2 * j * P:(2 * j + 2) * P, :].rearrange("(c p) n -> p c n", p=P)
                    dst = w_stage[:, j % 2, :].rearrange("p (c n) -> p c n", c=2)
                sp.dma_start(dst, src).then_inc(stage_loaded[j % 2], 16)

            def load_xT(c):
                t0, nt = CHUNKS[c]
                tokens = slice(t0 * P, (t0 + nt) * P)
                for part in range(2):
                    sp.dma_start(xT[:, part, :, tokens].bitcast(F32),
                                 xt_scratch.rearrange("s p c b q -> s p c (b q)")[part, :, :, tokens]
                                 ).then_inc(xT_loaded[c], 16)

            sp.wait_ge(in_psum["V"], number(("V", 0, 1, 5), B - 1))
            sp.wait_ge(in_psum["Q"], number(("Q", 0, 1, 1), B - 1))
            sp.wait_ge(in_psum["P"], number(("P", 0, G - 1), B - 1))
            load_piece(0, 1, 0, 0)
            load_piece(0, 1, 1, 1)
            sp.wait_ge(yT_stored, (B - 1) * 64)
            for c in range(3):
                load_xT(c)
            load_piece(0, 1, 2, 2)
            load_piece(0, 1, 3, 3)
            for qt in range(2):
                store_x2(B - 1, qt)
            for qt in range(2):
                store_yT(B - 1, qt)
            sp.wait_ge(att_lo, pair_number(B - 1, 3))
            for qt in range(2):
                sp.wait_ge(x2_stored[qt], B * 16)
            sp.wait_ge(yT_stored, B * 64)
            sp.dma_start(b1_rows, b1.rearrange("e (t p) -> (e t) p", p=P)).then_inc(small_loaded, 16)
            sp.dma_start(gate_rows, gate_w).then_inc(small_loaded, 16)
            sp.dma_start(b2_rows, b2).then_inc(small_loaded, 16)
            sp.dma_start(scaleb[:, 0, :], gate_b.partition_broadcast(P)).then_inc(scale_loaded, 16)
            sp.dma_start(scaleb[:, 1, :], rms_w.partition_broadcast(P)).then_inc(scale_loaded, 16)
            load_xT(3)

            with sp.Fori(0, NE - 1) as e:
                for j in range(4):
                    load_piece(e, 2, j, e * 8 + (4 + j))
                for j in range(4):
                    load_piece(e + 1, 1, j, e * 8 + (8 + j))
            for j in range(4):
                load_piece(NE - 1, 2, j, (NE - 1) * 8 + 4 + j)
            for t in range(TT):
                if t < 2:
                    sp.wait_ge(small_out, 3)
                else:
                    sp.wait_ge(out_stored[t % 2], 16 * (t // 2))
                sp.dma_start(x2_tile[:, t % 2, :], x2_scratch.rearrange("b q d -> (b q) d")[t * P:(t + 1) * P, :]
                             ).then_inc(x2_loaded[t % 2], 16)
                if t >= 1:
                    sp.wait_ge(out_ready, t)
                    sp.dma_start(out_rows[(t - 1) * P:t * P, :], x2_tile[:, (t - 1) % 2, :]
                                 ).then_inc(out_stored[(t - 1) % 2], 16)
            sp.wait_ge(out_ready, TT)
            sp.dma_start(out_rows[(TT - 1) * P:, :], x2_tile[:, (TT - 1) % 2, :]).then_inc(out_stored[(TT - 1) % 2], 16)
            for i in range(2):
                sp.wait_ge(out_stored[i], 16 * (TT // 2))

        @block.tensor
        def _(pe):
            def three(bank, parts, first=True, last=True):
                n, total = 0, 3 * len(parts)
                for s, m in parts:
                    for i, j in ((0, 0), (0, 1), (1, 0)):
                        mm = pe.matmul(bank, s[i], m[j], start=first and n == 0, stop=last and n == total - 1)
                        n += 1
                return mm

            def transposes(bank, tile, rows, cols):
                for c in range(KC):
                    t = pe.transpose(bank[:, c * rows:(c + 1) * rows], tile[0:rows, c * cols:(c + 1) * cols],
                                     ident[0:rows, 0:rows])
                return t

            def make(item, b, bank_table):
                kind = item[0]
                n = number(item, b) if kind not in ("END",) else None
                if kind in BANKED:
                    i, before = bank_table[item]
                    bank = ps[i]
                    if before is not None:
                        pe.wait_ge(lo_out[before[0]], number(before, b))
                db = item[1]
                if kind == "C":
                    t = item[2]
                    pe.wait_ge(ctx_loaded[t % 2], (b + db) * 48 + 16 * (t // 2 + 1))
                    last = transposes(bank, ctx_raw[:, t % 2, :], KT, P)
                elif kind == "X":
                    pe.wait_ge(ln_out, n_ln(0, b + db, item[2]))
                    last = transposes(bank, xa[:, item[2], :], QT, P)
                elif kind == "Y":
                    pe.wait_ge(ln_out, n_ln(1, b + db, item[2]))
                    last = transposes(bank, xa[:, item[2], :], QT, P)
                elif kind == "K":
                    _, _, g, p, half = item
                    k0, k1 = HALVES[half]
                    pe.wait_ge(lo_out["C"], number(("C", db, (k1 - 1) // KT), b))
                    cols = slice((2 * g + p) * P, (2 * g + p + 1) * P)
                    keys = slice(k0, k1)
                    last = three(bank[:, 0:k1 - k0], [([wk[:, s, c, cols] for s in range(2)],
                                                    [ctxT[:, s, c, keys] for s in range(2)]) for c in range(KC)])
                elif kind == "Q":
                    _, _, g, p = item
                    pe.wait_ge(lo_out["X"], number(("X", db, 1), b))
                    cols = slice((2 * g + p) * P, (2 * g + p + 1) * P)
                    last = three(bank[:, 0:NQ], [([wq[:, s, c, cols] for s in range(2)],
                                                  [xnT[:, s, c, :] for s in range(2)]) for c in range(KC)])
                elif kind == "V":
                    _, _, g, t = item
                    pe.wait_ge(lo_out["C"], number(("C", db, t), b))
                    keys = slice(t * KT, (t + 1) * KT)
                    cols = slice(g * G * DH, (g + 1) * G * DH)
                    last = three(bank[0:KT, 0:G * DH], [([ctxT[:, s, c, keys] for s in range(2)],
                                                         [wv[:, s, c, cols] for s in range(2)]) for c in range(KC)])
                elif kind == "S":
                    _, _, h, qt = item
                    g, hh = h // G, h % G
                    pe.wait_ge(lo_out["K"], number(("K", db, g, hh // 2, 1), b))
                    pe.wait_ge(lo_out["Q"], number(("Q", db, g, hh // 2), b))
                    if not (isinstance(b, int) and n <= 2):
                        pe.wait_ge(exp_out, n - 2)
                    rows = slice(qt * QT, (qt + 1) * QT)
                    for third in range(3):
                        for s in range(2):
                            last = pe.matmul(ps_scores[qt][0:QT, third, 0:SK], qst[g][:, s, hh, rows],
                                             kst[g][:, hh, third * SK:(third + 1) * SK], start=s == 0, stop=s == 1)
                elif kind == "T":
                    _, _, h, k = item
                    pe.wait_ge(probs_scaled, number(("R", db, h, 1), b))
                    for kt in range(2 * k, 2 * k + 2):
                        for qt in range(2):
                            at = (kt % 2) * NQ + qt * QT
                            last = pe.transpose(bank[0:KT, at:at + QT],
                                                probs[0:QT, (h % 2) * 2 + qt, kt * KT:(kt + 1) * KT],
                                                ident[0:QT, 0:QT])
                elif kind == "P":
                    h = item[2]
                    g, hh = h // G, h % G
                    odd = h % 2
                    pe.wait_ge(lo_out["V"], number(("V", db, g, NKT - 1), b))
                    if not (isinstance(b, int) and b == 0 and h < 2):
                        pe.wait_ge(pv_summed, b * 4 + h // 2)
                    for kt in range(NKT):
                        if kt % 2 == 0:
                            pe.wait_ge(lo_out["T"], number(("T", 0, h, kt // 2), b))
                        v = vst[g][0:KT, kt, hh // 2, 2 * odd:2 * odd + 2, :].rearrange("p s d -> p (s d)")
                        for s in range(2):
                            last = pe.matmul(ps_pv[:, odd * NQ:(odd + 1) * NQ], v,
                                             probsT[0:KT, s, kt // 2, (kt % 2) * NQ:(kt % 2 + 1) * NQ],
                                             start=kt == 0 and s == 0, stop=kt == NKT - 1 and s == 1)
                elif kind == "O":
                    qt = item[2]
                    pe.wait_ge(att_lo, pair_number(b + db, 3))
                    rows = slice(qt * QT, (qt + 1) * QT)
                    last = three(bank[0:QT, :], [([attT[:, s, c, rows] for s in range(2)],
                                                  [wo[:, s, c, :] for s in range(2)]) for c in range(KC)])
                else:
                    return
                last.then_inc(in_psum[kind], 1)

            pe.wait_ge(consts_set, 3)
            waited_w = set()
            for item in HEAD_PLAN:
                w = {"K": 0, "Q": 1, "V": 2}.get(item[0])
                if w is not None and w not in waited_w:
                    waited_w.add(w)
                    pe.wait_ge(w_lo, w + 1)
                make(item, 0, bank_of["head"])
            pe.wait_ge(w_lo, 4)

            def batch(name, plan, b):
                for item in plan:
                    if item[0] != "R":
                        make_or_skip(item, b, bank_of[name])

            def make_or_skip(item, b, table):
                if item[0] != "END":
                    make(item, b, table)

            batches(pe, batch)
            for item in TAIL_PLAN:
                make(item, B - 1, bank_of["tail"])

            pe.wait_ge(small_loaded, 48)
            pe.wait_ge(consts_set, 4)
            pe.wait_ge(lo_out["Y"], number(("Y", 0, 1), B - 1))
            pe.wait_ge(lo_out["O"], number(("O", 0, 1), B - 1))
            pe.transpose(ps[0][:, 0:NE * HT], b1_rows, ident[0:NE * HT, 0:NE * HT]).then_inc(small_psum, 1)
            for c in range(KC):
                t = pe.transpose(ps[1][:, c * NE:(c + 1) * NE], gate_rows[:, c * P:(c + 1) * P], ident[0:NE, 0:NE])
            t.then_inc(small_psum, 1)
            pe.matmul(ps[2][:, :], ones8, b2_rows, start=True, stop=True).then_inc(small_psum, 1)

            hb = [ps_scores[i // 2][:, 2 * (i % 2):2 * (i % 2) + 2, :].rearrange("p a n -> p (a n)") for i in range(4)]

            def ffn_in(e, c):
                t0, nt = CHUNKS[c]
                pe.wait_ge(piece_split, e * 8 + 4)
                for t in range(HT):
                    k = c * HT + t
                    if k >= 4:
                        pe.wait_ge(h_act, e * (4 * HT) + (k - 3))
                    three(hb[t % 4][:, 0:nt * P],
                          [([w1s[:, s, kc, t * P:(t + 1) * P] for s in range(2)],
                            [xT[:, s, kc, t0 * P:(t0 + nt) * P] for s in range(2)]) for kc in range(KC)]
                          ).then_inc(h_psum, 1)

            def ffn_out(e, c):
                t0, nt = CHUNKS[c]
                for t in range(nt):
                    k = t0 + t
                    if k >= 2:
                        pe.wait_ge(y_added, e * TT + (k - 1))
                    for ht in range(HT):
                        if t == 0:
                            pe.wait_ge(h_split, e * (4 * HT) + (c * HT + ht + 1))
                        if k == 0 and ht % 2 == 0:
                            pe.wait_ge(piece_split, e * 8 + (5 + ht // 2))
                        mm = three(ps[k % 2][:, :], [([hs[:, s, ht, t * P:(t + 1) * P] for s in range(2)],
                                                      [w2s[:, s, ht, :] for s in range(2)])],
                                   first=ht == 0, last=ht == HT - 1)
                    mm.then_inc(y_psum, 1)

            def expert(e, extra=None):
                for c in range(len(CHUNKS)):
                    ffn_in(e, c)
                    ffn_out(e, c)

            for c in range(len(CHUNKS)):
                pe.wait_ge(xT_loaded[c], 32)
            pe.wait_ge(small_out, 3)
            pe.wait_ge(exp_out, 16 * B)
            with pe.Fori(0, NE - 1) as e:
                expert(e)
            e = NE - 1
            for c, (t0, nt) in enumerate(CHUNKS):
                pe.wait_ge(h_act, e * 4 * HT - 3 + c)
                for kc in range(KC):
                    for s in range(2):
                        mm = pe.matmul(hb[c][:, 0:nt * P], gate_st[:, kc, :], xT[:, s, kc, t0 * P:(t0 + nt) * P],
                                       start=kc == 0 and s == 0, stop=kc == KC - 1 and s == 1)
                mm.then_inc(gate_psum, 1)
            pe.wait_ge(y_added, e * TT)
            for c, (t0, nt) in enumerate(CHUNKS):
                pe.wait_ge(gate_copied, c + 1)
                for t in range(nt):
                    tr = pe.transpose(ps[2][:, (t0 + t) * 16:(t0 + t + 1) * 16],
                                      h_full[0:16, c % 2, t * P:(t + 1) * P], ident[0:16, 0:16])
                tr.then_inc(gate_tr, 1)
            expert(e)

        @block.vector
        def _(dve):
            def split_w(i, w):
                dve.wait_ge(w_hi, i + 1)
                dve.tensor_tensor(w[:, 1], w_raw[:, i], w[:, 0].bitcast(F32), ALU.subtract).then_inc(w_lo, 1)

            def lnorm_stats(which, b, src, slot):
                n = n_ln(which, b, slot % 2)
                dve.bn_stats(stats[0:QT, slot, :], src).then_inc(ln_step, 1)
                dve.wait_ge(ln_step, n * 2 - 1)
                alone(dve, passed["dve"])
                dve.bn_aggr(mean_var[0:QT, slot, :], stats[0:QT, slot, :]).then_inc(ln_step, 1)
                dve.wait_ge(ln_step, n * 2)
                dve.tensor_scalar(rstd[0:QT, slot:slot + 1], mean_var[0:QT, slot, 1:2], LN_EPS, None,
                                  ALU.add).then_inc(ln_var, 1)

            def lnorm_apply(which, b, src, dst, slot):
                dve.wait_ge(ln_rstd, n_ln(which, b, slot % 2))
                dve.tensor_scalar(dst, src, mean_var[0:QT, slot, 0:1], rstd[0:QT, slot:slot + 1],
                                  ALU.subtract, ALU.mult).then_inc(ln_out, 1)

            def load_norm_x(b, qt):
                dve.wait_ge(x_loaded[qt], b * 16 + 16)
                lnorm_stats(0, b, xa[0:QT, qt, :], qt)
                lnorm_apply(0, b, xa[0:QT, qt, :], xa[0:QT, qt, :], qt)

            def sub(out, a_, b_):
                return dve.tensor_tensor(out, a_, b_.bitcast(F32), ALU.subtract)

            def drain(item, b, bank_table):
                kind, db = item[0], item[1]
                if kind in ("R", "END", "P", "S", "O"):
                    return special(item, b, bank_table)
                bank = ps[bank_table[item][0]]
                n = number(item, b)
                dve.wait_ge(hi_out[kind], n)
                if kind == "C":
                    t = item[2]
                    cols = slice(t * KT, (t + 1) * KT)
                    last = sub(ctxT[:, 1, :, cols], bank[:, 0:KC * KT].rearrange("p (c k) -> p c k", c=KC),
                               ctxT[:, 0, :, cols])
                elif kind == "X":
                    cols = slice(item[2] * QT, (item[2] + 1) * QT)
                    last = sub(xnT[:, 1, :, cols], bank[:, 0:KC * QT].rearrange("p (c k) -> p c k", c=KC),
                               xnT[:, 0, :, cols])
                elif kind == "Y":
                    last = sub(yT[:, 1], bank[:, 0:KC * QT].rearrange("p (c k) -> p c k", c=KC), yT[:, 0])
                elif kind == "K":
                    _, _, g, p, half = item
                    keys = slice(*HALVES[half])
                    n = keys.stop - keys.start
                    sub(kst[g][64:128, 2 * p, keys], bank[0:64, 0:n], kst[g][0:64, 2 * p, keys])
                    last = sub(kst[g][0:64, 2 * p + 1, keys], bank[64:128, 0:n], kst[g][64:128, 2 * p + 1, keys])
                elif kind == "Q":
                    _, _, g, p = item
                    for odd in range(2):
                        src = slice(64 * odd, 64 * odd + 64)
                        for to in range(2):
                            last = dve.scalar_tensor_tensor(
                                qst[g][64 * to:64 * to + 64, 1, 2 * p + odd, :], bank[src, 0:NQ], DH ** -0.5,
                                qst[g][src, 0, 2 * p + odd, :].bitcast(F32), ALU.mult, ALU.subtract)
                elif kind == "V":
                    _, _, g, t = item
                    last = sub(vst[g][0:KT, t, :, 1:3, :],
                               bank[0:KT, 0:G * DH].rearrange("p (a s d) -> p a s d", a=2, s=2),
                               vst[g][0:KT, t, :, 0::3, :])
                elif kind == "T":
                    k = item[3]
                    last = sub(probsT[0:KT, 1, k, :], bank[0:KT, 0:2 * NQ], probsT[0:KT, 0, k, :])
                last.then_inc(lo_out[kind], 1)

            def special(item, b, bank_table):
                kind, db = item[0], item[1]
                if kind == "S":
                    _, _, h, qt = item
                    i = (h % 2) * 2 + qt
                    dve.wait_ge(in_psum["S"], number(item, b))
                    dve.tensor_reduce(neg_max[0:QT, i:i + 1], ps_scores[qt][0:QT, 0:3, 0:SK], AX.XY, ALU.max,
                                      negate=True).then_inc(max_out, 1)
                elif kind == "R":
                    _, _, h, qt = item
                    i = (h % 2) * 2 + qt
                    dve.wait_ge(exp_out, number(item, b))
                    dve.reciprocal(row_inv[0:QT, i:i + 1], row_sum[0:QT, i:i + 1]).then_inc(inv_out, 1)
                elif kind == "P" and item[2] % 2:
                    pair = pair_number(b, item[2] // 2)
                    dve.wait_ge(pv_swapped, pair)
                    if not (isinstance(b, int) and b == 0 and item[2] == 1):
                        dve.wait_ge(att_lo, pair - 1)
                    for odd in range(2):
                        rows = slice(64 * odd, 64 * odd + 64)
                        last = dve.tensor_tensor(att_sum[rows, :], ps_pv[rows, odd * NQ:(odd + 1) * NQ],
                                                 att_tmp[rows, :], ALU.add)
                    last.then_inc(pv_summed, 1)
                elif kind == "O":
                    qt = item[2]
                    n = number(item, b)
                    dve.wait_ge(in_psum["O"], n)
                    dve.wait_ge(xres_biased, n)
                    dve.scalar_tensor_tensor(xres[0:QT, qt, :], ps[bank_table[item][0]][0:QT, :], tanh_g[0:QT, 0:1],
                                             xres[0:QT, qt, :], ALU.mult, ALU.add).then_inc(lo_out["O"], 1)
                    dve.wait_ge(lo_out["O"], n)
                    lnorm_stats(1, b + db, xres[0:QT, qt, :], 2 + qt)
                    lnorm_apply(1, b + db, xres[0:QT, qt, :], xa[0:QT, qt, :], 2 + qt)

            dve.wait_ge(consts_set, 3)
            for qt in range(2):
                load_norm_x(0, qt)
            todo = [wk, wq, wv, wo]
            k = 0
            for item in HEAD_PLAN:
                if item in (("K", 0, 0, 0, 0), ("Q", 0, 0, 0), ("V", 0, 0, 0)):
                    pass
                if item in (("X", 0, 0), ("X", 0, 1), ("K", 0, 0, 0, 1), ("K", 0, 0, 1, 1)):
                    split_w(k, todo[k])
                    k += 1
                drain(item, 0, bank_of["head"])
            dve.wait_ge(bo_loaded, 16)
            dve.wait_ge(tanh_done, 1)
            dve.tensor_scalar(bo_t[:, :], bo_t[:, :], tanh_g[:, 0:1], None, ALU.mult).then_inc(bo_scaled, 1)

            def split_piece(e, which, j, n):
                dve.wait_ge(stage_loaded[j % 2], e * 64 + (16 * (j // 2 + 1) + 32 * (which - 1)))
                if which == 1:
                    dst = [w1s[:, s, j, :] for s in range(2)]
                else:
                    dst = [w2s[:, s, 2 * j:2 * j + 2, :].rearrange("p c n -> p (c n)") for s in range(2)]
                dve.tensor_copy(dst[0], w_stage[:, j % 2, :]).then_inc(piece_hi, 1)
                dve.wait_ge(piece_hi, n + 1)
                sub(dst[1], w_stage[:, j % 2, :], dst[0]).then_inc(piece_split, 1)

            def batch(name, plan, b):
                for item in plan:
                    drain(item, b, bank_of[name])
                    if item[0] == "END" and item[2] in (3, 4) and name != "last":
                        load_norm_x(b + 1, item[2] - 3)
                    if item[0] == "END" and item[2] >= 4 and name == "last":
                        split_piece(0, 1, item[2] - 4, item[2] - 4)

            batches(dve, batch)
            for item in TAIL_PLAN:
                drain(item, B - 1, bank_of["tail"])

            dve.memset(gate_st[:, :, :].bitcast(F32), 0.0).then_inc(small_out, 1)
            dve.wait_ge(small_psum, 1)
            dve.tensor_copy(b1T[:, :], ps[0][:, 0:NE * HT]).then_inc(small_out, 1)
            dve.wait_ge(small_psum, 2)
            dve.wait_ge(small_out, 1)
            gw = ps[1][:, 0:KC * NE].rearrange("p (c n) -> p c n", c=KC)
            dve.tensor_copy(gate_st[:, :, 0:NE], gw).then_inc(gate_step, 1)
            dve.wait_ge(gate_step, 1)
            dve.wait_ge(acc_set, TT)
            sub(gate_st[:, :, NE:2 * NE], gw, gate_st[:, :, 0:NE]).then_inc(small_out, 1)

            def hidden(e, c, with_w2):
                t0, nt = CHUNKS[c]
                for t in range(HT):
                    k = c * HT + t
                    dve.wait_ge(h_act, e * (4 * HT) + (k + 1))
                    sub(hs[:, 1, t, 0:nt * P], h_full[:, t % 2, 0:nt * P], hs[:, 0, t, 0:nt * P]).then_inc(h_split, 1)
                    if with_w2 and t % 2 == 0:
                        split_piece(e, 2, t // 2, e * 8 + (4 + t // 2))

            def add_up(e, k):
                dve.wait_ge(y_psum, e * TT + (k + 1))
                dve.tensor_tensor(acc[:, k, :], ps[k % 2][:, :], acc[:, k, :], ALU.add).then_inc(y_added, 1)

            with dve.Fori(0, NE - 1) as e:
                for c, (t0, nt) in enumerate(CHUNKS):
                    hidden(e, c, c == 0)
                    for t in range(nt):
                        if c == 3:
                            if t == 0:
                                dve.wait_ge(h_psum, e * (4 * HT) + 4 * HT)
                                split_piece(e + 1, 1, 0, e * 8 + 8)
                                split_piece(e + 1, 1, 1, e * 8 + 9)
                            elif t == 1:
                                split_piece(e + 1, 1, 2, e * 8 + 10)
                                split_piece(e + 1, 1, 3, e * 8 + 11)
                        add_up(e, t0 + t)

            e = NE - 1
            step = [1]

            def chain(ins):
                ins.then_inc(gate_step, 1)
                step[0] += 1
                dve.wait_ge(gate_step, step[0])

            dve.wait_ge(gate_tr, 4)
            dve.wait_ge(scale_loaded, 32)
            pair = ps[2][:, 0:TT * 16].rearrange("p (t n) -> p t n", t=TT)
            chain(dve.tensor_copy(lg_lo[:, :, :], pair[:, :, NE:2 * NE]))
            chain(dve.tensor_tensor(logits[:, :, :], pair[:, :, 0:NE], lg_lo[:, :, :], ALU.add))
            chain(dve.tensor_tensor(logits[:, :, :], logits[:, :, :],
                                    scaleb[:, 0:1, :].to_broadcast([P, TT, NE]), ALU.add))
            chain(dve.tensor_tensor(lg_lo[:, :, :], logits[:, :, :], logits[:, :, :], ALU.mult))
            chain(dve.tensor_reduce(gate_small[:, 0, :], lg_lo[:, :, :], AX.X, ALU.add))
            chain(dve.tensor_scalar(gate_small[:, 1, :], gate_small[:, 0, :], 1.0 / NE, RMS_EPS, ALU.mult, ALU.add))
            dve.wait_ge(gate_pow, 1)
            chain(dve.tensor_tensor(logits[:, :, :], logits[:, :, :],
                                    gate_small[:, 2, :].unsqueeze(2).to_broadcast([P, TT, NE]), ALU.mult))
            chain(dve.tensor_tensor(logits[:, :, :], logits[:, :, :],
                                    scaleb[:, 1:2, :].to_broadcast([P, TT, NE]), ALU.mult))
            chain(dve.tensor_reduce(gate_small[:, 3, :], logits[:, :, :], AX.X, ALU.max))
            chain(dve.tensor_tensor(logits[:, :, :], logits[:, :, :],
                                    gate_small[:, 3, :].unsqueeze(2).to_broadcast([P, TT, NE]), ALU.subtract))
            gate_ready_for_exp = step[0]
            hidden(e, 0, True)
            dve.wait_ge(gate_exp, 1)
            chain(dve.tensor_reduce(gate_small[:, 0, :], lg_lo[:, :, :], AX.X, ALU.add))
            chain(dve.reciprocal(gate_small[:, 1, :], gate_small[:, 0, :]))
            chain(dve.tensor_scalar(gate_small[:, 3, :], gate_small[:, 1, :], NORM_EPS, None, ALU.add))
            chain(dve.reciprocal(gate_small[:, 4, :], gate_small[:, 3, :]))
            chain(dve.tensor_tensor(gate_small[:, 5, :], gate_small[:, 1, :], gate_small[:, 4, :], ALU.mult))
            chain(dve.tensor_scalar(token_gate[:, :], gate_small[:, 5, :], tanh_g[:, 1:2], None, ALU.mult))
            for c, (t0, nt) in enumerate(CHUNKS):
                if c:
                    hidden(e, c, False)
                for t in range(nt):
                    k = t0 + t
                    add_up(e, k)
                    dve.wait_ge(y_added, e * TT + k + 1)
                    dve.wait_ge(x2_loaded[k % 2], 16 * (k // 2 + 1))
                    dve.scalar_tensor_tensor(x2_tile[:, k % 2, :], acc[:, k, :], token_gate[:, k:k + 1],
                                             x2_tile[:, k % 2, :], ALU.mult, ALU.add).then_inc(out_ready, 1)

        @block.scalar
        def _(act):
            def copy(dst, src, scale=1.0):
                return act.activation(dst, src, ACT.Copy, scale=scale)

            def hi(item, b, bank_table):
                kind, db = item[0], item[1]
                if kind in ("R", "END", "O"):
                    return
                n = number(item, b)
                if kind == "S":
                    _, _, h, qt = item
                    i = (h % 2) * 2 + qt
                    act.wait_ge(max_out, n)
                    if not (isinstance(b, int) and n <= 4):
                        act.wait_ge(in_psum["T"], number(("T", db, h, 2), b) - 6)
                        act.wait_ge(inv_out, n - 4)
                    act.activation(probs[0:QT, i, :].rearrange("p (a k) -> p a k", a=3),
                                   ps_scores[qt][0:QT, 0:3, 0:SK], ACT.Exp, bias=neg_max[0:QT, i:i + 1],
                                   accum_out=row_sum[0:QT, i:i + 1]).then_inc(exp_out, 1)
                    return
                if kind == "P":
                    if item[2] % 2:
                        pair = pair_number(b, item[2] // 2)
                        act.wait_ge(in_psum["P"], n)
                        if not (isinstance(b, int) and b == 0 and item[2] == 1):
                            act.wait_ge(pv_summed, pair - 1)
                        copy(att_tmp[0:64, :], ps_pv[64:128, 0:NQ])
                        copy(att_tmp[64:128, :], ps_pv[0:64, NQ:2 * NQ]).then_inc(pv_swapped, 1)
                    return
                bank = ps[bank_table[item][0]]
                act.wait_ge(in_psum[kind], n)
                if kind == "C":
                    t = item[2]
                    if db:
                        act.wait_ge(in_psum["K"], number(("K", 0, 1, 1, 1), b))
                        act.wait_ge(in_psum["V"], number(("V", 0, 1, 5), b))
                    last = copy(ctxT[:, 0, :, t * KT:(t + 1) * KT],
                                bank[:, 0:KC * KT].rearrange("p (c k) -> p c k", c=KC))
                elif kind == "X":
                    if db:
                        act.wait_ge(in_psum["Q"], number(("Q", 0, 1, 1), b))
                    cols = slice(item[2] * QT, (item[2] + 1) * QT)
                    last = copy(xnT[:, 0, :, cols], bank[:, 0:KC * QT].rearrange("p (c k) -> p c k", c=KC))
                elif kind == "Y":
                    if item[2] == 1:
                        act.wait_ge(yT_stored, (b + db) * 64 + 32)
                    elif not (isinstance(b, int) and b + db == 0):
                        act.wait_ge(yT_stored, (b + db) * 64)
                    last = copy(yT[:, 0], bank[:, 0:KC * QT].rearrange("p (c k) -> p c k", c=KC))
                elif kind == "K":
                    _, _, g, p, half = item
                    keys = slice(*HALVES[half])
                    n = keys.stop - keys.start
                    copy(kst[g][0:64, 2 * p, keys], bank[0:64, 0:n])
                    last = copy(kst[g][64:128, 2 * p + 1, keys], bank[64:128, 0:n])
                elif kind == "Q":
                    _, _, g, p = item
                    for odd in range(2):
                        for to in range(2):
                            last = copy(qst[g][64 * to:64 * to + 64, 0, 2 * p + odd, :],
                                        bank[64 * odd:64 * odd + 64, 0:NQ], scale=DH ** -0.5)
                elif kind == "V":
                    _, _, g, t = item
                    last = copy(vst[g][0:KT, t, :, 0::3, :],
                                bank[0:KT, 0:G * DH].rearrange("p (a s d) -> p a s d", a=2, s=2))
                elif kind == "T":
                    k = item[3]
                    last = copy(probsT[0:KT, 0, k, :], bank[0:KT, 0:2 * NQ])
                last.then_inc(hi_out[kind], 1)

            act.wait_ge(g_loaded, 32)
            act.activation(tanh_g[:, :], tanh_g[:, :], ACT.Tanh).then_inc(tanh_done, 1)
            order = {("C", 0, 2): (0, wk), ("C", 0, 4): (1, wq), ("X", 0, 1): (2, wv), ("K", 0, 0, 0, 0): (3, wo)}
            for item in HEAD_PLAN:
                hi(item, 0, bank_of["head"])
                if item in order:
                    i, w = order[item]
                    act.wait_ge(w_loaded[i], 16)
                    copy(w[:, 0], w_raw[:, i]).then_inc(w_hi, 1)

            batches(act, lambda name, plan, b: [hi(item, b, bank_of[name]) for item in plan])
            for item in TAIL_PLAN:
                hi(item, B - 1, bank_of["tail"])

            act.wait_ge(small_psum, 3)
            for t in range(TT):
                copy(acc[:, t, :], ps[2][:, :]).then_inc(acc_set, 1)
            act.wait_ge(small_out, 3)

            hb = [ps_scores[i // 2][:, 2 * (i % 2):2 * (i % 2) + 2, :].rearrange("p a n -> p (a n)") for i in range(4)]

            def gelu(e, c):
                t0, nt = CHUNKS[c]
                for t in range(HT):
                    k = c * HT + t
                    act.wait_ge(h_psum, e * (4 * HT) + (k + 1))
                    if k >= 2:
                        act.wait_ge(h_split, e * (4 * HT) + (k - 1))
                    alone(act, passed["act"])
                    bias = b1T[:, bass.ds(e * HT + t, 1)]
                    act.activation(h_full[:, t % 2, 0:nt * P], hb[t % 4][:, 0:nt * P], ACT.Gelu, bias=bias)
                    act.activation(hs[:, 0, t, 0:nt * P], hb[t % 4][:, 0:nt * P], ACT.Gelu,
                                   bias=bias).then_inc(h_act, 1)

            with act.Fori(0, NE - 1) as e:
                for c in range(len(CHUNKS)):
                    gelu(e, c)
            e = NE - 1
            for c, (t0, nt) in enumerate(CHUNKS):
                act.wait_ge(gate_psum, c + 1)
                act.wait_ge(h_split, e * 4 * HT)
                if c >= 2:
                    act.wait_ge(gate_tr, c - 1)
                copy(h_full[0:16, c % 2, 0:nt * P], hb[c][0:16, 0:nt * P]).then_inc(gate_copied, 1)
            act.wait_ge(gate_tr, 4)
            gelu(e, 0)
            act.wait_ge(gate_step, 11)
            act.activation(lg_lo[:, :, :], logits[:, :, :], ACT.Exp, scale=1.0 / TEMPERATURE).then_inc(gate_exp, 1)
            for c in range(1, len(CHUNKS)):
                gelu(e, c)

        @block.gpsimd
        def _(pool):
            pool.memset(ident[:, :], 0.0).then_inc(consts_set, 1)
            pool.wait_ge(consts_set, 1)
            pool.affine_select(out=ident[:, :], in_=ident[:, :], compare_op=ALU.not_equal, fill=1.0, base=0,
                               pattern=[[-1, P]], channel_multiplier=1).then_inc(consts_set, 1)
            pool.memset(minus_half[:, :], -0.5).then_inc(consts_set, 1)
            pool.wait_ge(consts_set, 3)

            def inv_sqrt(which, b, slot):
                pool.wait_ge(ln_var, n_ln(which, b, slot % 2))
                pool.tensor_tensor(rstd[0:QT, slot:slot + 1], rstd[0:QT, slot:slot + 1], minus_half[0:QT, 0:1],
                                   ALU.pow).then_inc(ln_rstd, 1)

            def handle(item, b):
                kind, db = item[0], item[1]
                if kind == "R":
                    _, _, h, qt = item
                    i = (h % 2) * 2 + qt
                    pool.wait_ge(inv_out, number(item, b))
                    alone(pool, passed["pool"])
                    pool.tensor_scalar(probs[0:QT, i, :], probs[0:QT, i, :], row_inv[0:QT, i:i + 1], None,
                                       ALU.mult).then_inc(probs_scaled, 1)
                elif kind == "P" and item[2] % 2:
                    pair = item[2] // 2
                    n = pair_number(b, pair)
                    pool.wait_ge(pv_summed, n)
                    if pair == 0 and not (isinstance(b, int) and b == 0):
                        pool.wait_ge(in_psum["O"], b * 2)
                    alone(pool, passed["pool"])
                    pool.tensor_copy(attT[:, 0, pair, :], att_sum[:, :]).then_inc(att_hi, 1)
                    pool.wait_ge(att_hi, n)
                    pool.tensor_tensor(attT[:, 1, pair, :], att_sum[:, :], attT[:, 0, pair, :].bitcast(F32),
                                       ALU.subtract).then_inc(att_lo, 1)
                elif kind == "O":
                    inv_sqrt(1, b + db, 2 + item[2])

            def bias_x(b):
                pool.wait_ge(bo_scaled, 1)
                for qt in range(2):
                    pool.wait_ge(xres_loaded[qt], b * 16 + 16)
                    pool.tensor_tensor(xres[0:QT, qt, :], xres[0:QT, qt, :], bo_t[0:QT, :],
                                       ALU.add).then_inc(xres_biased, 1)

            for qt in range(2):
                inv_sqrt(0, 0, qt)
            for item in HEAD_PLAN:
                handle(item, 0)

            def batch(name, plan, b):
                for item in plan:
                    handle(item, b)
                    if item[0] == "END" and item[2] in (3, 4) and name != "last":
                        inv_sqrt(0, b + 1, item[2] - 3)
                    if item[0] == "END" and item[2] == 2:
                        bias_x(b)

            batches(pool, batch)
            for item in TAIL_PLAN:
                handle(item, B - 1)

            pool.wait_ge(small_loaded, 48)
            pool.memset(ones8, 1.0).then_inc(consts_set, 1)
            pool.wait_ge(gate_step, 7)
            pool.tensor_tensor(gate_small[:, 2, :], gate_small[:, 1, :], minus_half[:, 0:TT],
                               ALU.pow).then_inc(gate_pow, 1)


def n_ln(which, b, qt):
    if which == 0:
        if isinstance(b, int) and b == 0:
            return qt + 1
        return b * 4 + (qt - 1)
    if isinstance(b, int) and b == B - 1:
        return 4 * B - 2 + qt + 1
    return b * 4 + (qt + 5)


_INS = ['x', 'ctx_1024', 'g_xattn', 'g_ffn', 'L0_xattn_Wq', 'L0_xattn_Wk', 'L0_xattn_Wv', 'L0_xattn_Wo',
        'L0_xattn_bo', 'L0_ffn_gate_w', 'L0_ffn_gate_b', 'L0_ffn_rms_w', 'L0_ffn_w1', 'L0_ffn_b1', 'L0_ffn_w2',
        'L0_ffn_b2']


def kernel(**inputs):
    import numpy as _np
    import concourse.bacc as _bacc
    from concourse import mybir as _mybir
    from concourse.bass_utils import run_bass_kernel_spmd as _run

    nc = _bacc.Bacc("TRN2", target_bir_lowering=False, num_devices=1)
    arrays, args = {}, []
    for name in _INS:
        a = _np.ascontiguousarray(inputs[name])
        arrays[f"in_{name}"] = a
        args.append(nc.dram_tensor(f"in_{name}", a.shape, _mybir.dt.from_np(a.dtype), kind="ExternalInput").ap())
    args.append(nc.dram_tensor("out_0", (B, NQ, D), F32, kind="ExternalOutput").ap())
    args.append(nc.dram_tensor("x2_scratch", (B, NQ, D), F32, kind="Internal").ap())
    args.append(nc.dram_tensor("xt_scratch", (2, P, KC, B, NQ), F32, kind="Internal").ap())
    flamingo_kernel(nc, *args)
    r = _run(nc, [arrays], core_ids=[0])
    return r.results[0]["out_0"]
```

```python
from contextlib import ExitStack

import concourse.bass as bass
from concourse import mybir

ALU = mybir.AluOpType
ACT = mybir.ActivationFunctionType
F32 = mybir.dt.float32
F32R = mybir.dt.float32r
AX = mybir.AxisListType

P = 128
B, NQ, D = 8, 224, 512
NK = 750
H, DH = 8, 64
G = 4
KC = D // P
QT = NQ // 2
KT = NK // 6
NKT = NK // KT
CR = 3
SK = NK // 3
HALVES = [(0, 376), (376, NK)]
N = B * NQ
NE, HID = 8, 1024
HT = HID // P
TT = N // P
CHUNKS = [(0, 4), (4, 4), (8, 3), (11, 3)]
LN_EPS = 1e-5
RMS_EPS = 1.1920928955078125e-07
TEMPERATURE = 0.5
NORM_EPS = 1e-6


def number(item, b):
    kind, db = item[0], item[1]
    n = b + db
    if kind == "B":
        return item[2] + 1
    if kind == "C":
        return n * NKT + (item[2] + 1)
    if kind in ("X", "O", "Y"):
        return n * 2 + (item[2] + 1)
    if kind == "K":
        return n * 8 + (item[2] * 4 + item[3] * 2 + item[4] + 1)
    if kind == "Q":
        return n * 4 + (item[2] * 2 + item[3] + 1)
    if kind == "V":
        return n * 12 + (item[2] * 6 + item[3] + 1)
    if kind == "T":
        return n * 24 + (item[2] * 3 + item[3] + 1)
    if kind in "SRM":
        return n * 16 + (item[2] * 2 + item[3] + 1)
    assert kind in "PD"
    return n * 8 + (item[2] + 1)


SCALER = ("act", "pool")
BANKED = "CXKQVTOYPB"
RING = 4

FILL = [
    [[("K", 0, 1, 0, 0), ("Q", 0, 1, 0)], [("K", 0, 1, 0, 1)], [], [("O", -1, 0)]],
    [[], [], [("K", 0, 1, 1, 0)], [("O", -1, 1), ("V", 0, 1, 0), ("Y", -1, 0), ("K", 0, 1, 1, 1), ("V", 0, 1, 1)]],
    [[], [], [("V", 0, 1, 2)], []],
    [[("V", 0, 1, 3)], [("V", 0, 1, 4), ("Y", -1, 1), ("C", 1, 0), ("Q", 0, 1, 1)], [("C", 1, 1)], [("V", 0, 1, 5)]],
    [[], [("V", 1, 0, 0), ("C", 1, 2), ("C", 1, 3), ("C", 1, 4)],
     [("X", 1, 0)], [("V", 1, 0, 1), ("K", 1, 0, 0, 0), ("V", 1, 0, 2)]],
    [[("X", 1, 1)], [("C", 1, 5)], [], []],
    [[("K", 1, 0, 0, 1)], [("Q", 1, 0, 0)], [("K", 1, 0, 1, 0)], [("V", 1, 0, 3), ("K", 1, 0, 1, 1)]],
    [[], [("Q", 1, 0, 1)], [("V", 1, 0, 4), ("V", 1, 0, 5)], []],
]
NORMS = {
    ("O", -1, 0): [("L", -1, 1, 0)],
    ("O", -1, 1): [("L", -1, 1, 1)],
    ("T", 0, 1, 0): [("A", -1, 1, 0)],
    ("T", 0, 2, 0): [("A", -1, 1, 1)],
    ("T", 0, 3, 0): [("L", 1, 0, 0)],
    ("P", 0, 3): [("A", 1, 0, 0)],
    ("T", 0, 4, 1): [("L", 1, 0, 1)],
    ("T", 0, 4, 2): [("A", 1, 0, 1)],
}

STEPS = "D F0 T0 F1 R0 R1 F2 T1 T2 M0 M1 S0 S1 F3 P"


def body_plan(first, last):
    plan = []
    for h in range(H):
        fill = FILL[h]
        nxt = (0, h + 2) if h < H - 2 else (1, h + 2 - H)
        inv = (0, h + 1) if h < H - 1 else (1, 0)
        step = {"S0": [("S", *nxt, 0)], "S1": [("S", *nxt, 1)], "R0": [("R", *inv, 0)], "R1": [("R", *inv, 1)],
                "M0": [("M", *inv, 0)], "M1": [("M", *inv, 1)],
                "D": [("D", 0, h - 1) if h else ("D", -1, H - 1)], "P": [("P", 0, h)]}
        for i in range(3):
            step[f"T{i}"] = [("T", 0, h, i)]
        for i in range(4):
            step[f"F{i}"] = fill[i]
        items = sum((step[i] for i in STEPS.split()), [])
        for item in items:
            plan += [item] + NORMS.get(item, [])
        if last and h >= G:
            plan.append(("W", 0, h - G))
            plan += {G: [("Z", 0)], G + 2: [("B", 0, 0), ("B", 0, 1), ("B", 0, 2)]}.get(h, [])
    return [i for i in plan if not (first and i[1] < 0) and not (last and i[1] > 0)]


HEAD_PLAN = [("L", 0, 0, 0), ("L", 0, 0, 1), ("A", 0, 0, 0), ("A", 0, 0, 1), ("C", 0, 0), ("C", 0, 1), ("X", 0, 0),
             ("C", 0, 2), ("X", 0, 1), ("C", 0, 3), ("C", 0, 4), ("K", 0, 0, 0, 0), ("C", 0, 5), ("K", 0, 0, 0, 1),
             ("Q", 0, 0, 0), ("K", 0, 0, 1, 0), ("S", 0, 0, 0), ("S", 0, 0, 1), ("V", 0, 0, 0), ("V", 0, 0, 1),
             ("K", 0, 0, 1, 1), ("M", 0, 0, 0), ("M", 0, 0, 1), ("R", 0, 0, 0), ("R", 0, 0, 1), ("Q", 0, 0, 1),
             ("S", 0, 1, 0), ("V", 0, 0, 2), ("V", 0, 0, 3), ("S", 0, 1, 1), ("V", 0, 0, 4), ("V", 0, 0, 5)]
SPLIT_AT = [("X", 0, 0), ("C", 0, 3)]
TAIL_PLAN = ([("D", 0, H - 1), ("H", 0, 0), ("O", 0, 0), ("L", 0, 1, 0), ("O", 0, 1), ("H", 0, 1), ("L", 0, 1, 1),
              ("A", 0, 1, 0), ("A", 0, 1, 1), ("H", 0, 2), ("Y", 0, 0), ("Y", 0, 1)]
             + [("H", 0, t) for t in range(3, HT)])


def banks(plan, before):
    def in_turn(items):
        items = [i for i in items if i[0] in BANKED]
        return [((n - len(items)) % RING, i) for n, i in enumerate(items)]

    last = {bank: item for bank, item in in_turn(before)}
    out = {}
    for bank, item in in_turn(plan):
        out[item] = (bank, last.get(bank))
        last[bank] = item
    return out


def shifted(plan, d):
    return [(i[0], i[1] + d, *i[2:]) for i in plan]


def alone(eng, waits_passed):
    eng.sem_inc(waits_passed, 1)


def flamingo_kernel(nc, x, ctx, g_xattn, g_ffn, Wq, Wk, Wv, Wo, bo, gate_w, gate_b, rms_w, w1, b1, w2, b2, out,
                    x2_scratch, xt_scratch):
    FIRST, MIDDLE, LAST = body_plan(True, False), body_plan(False, False), body_plan(False, True)
    bank_of = {
        "head": banks(HEAD_PLAN, []),
        "first": banks(FIRST, HEAD_PLAN),
        "middle": banks(MIDDLE, shifted(MIDDLE, -1)),
        "last": banks(LAST, shifted(MIDDLE, -1)),
        "tail": banks(TAIL_PLAN, LAST),
    }

    out_rows = out.rearrange("b q d -> (b q) d")

    with ExitStack() as st:
        def sem(name):
            return st.enter_context(nc.semaphore(name))

        def alloc(stack, name, shape, dt=F32):
            return stack.enter_context(nc.sbuf_tensor(name, shape, dt))

        ident = alloc(st, "ident", [P, P])
        tanh_g = alloc(st, "tanh_g", [P, 2])
        minus_half = alloc(st, "minus_half", [P, 16])
        ps = [st.enter_context(nc.psum_tensor(f"bank{i}", [P, 512], F32)) for i in range(RING)]
        ps_scores = [st.enter_context(nc.psum_tensor(f"scores{i}", [P, 4, 256], F32)) for i in range(2)]

        with ExitStack() as att:
            def a(name, shape, dt=F32):
                return alloc(att, name, shape, dt)

            wk = a("wk", [P, 2, KC, D], F32R)
            wv = a("wv", [P, 2, KC, D], F32R)
            ctxT = a("ctxT", [P, 2, KC, NK], F32R)
            wq = a("wq", [P, 2, KC, D], F32R)
            kst, vst, qst = [None] * 2, [None] * 2, [None] * 2
            kst[0] = a("keys0", [P, G, NK], F32R)
            vst[0] = a("values0", [P, NKT, G // 2, 4, DH], F32R)
            qst[0] = a("queries0", [P, 2, G, NQ], F32R)
            ctx_raw = a("ctx_raw", [P, CR, D])
            xnT = a("xnT", [P, 2, KC, NQ], F32R)
            kst[1] = a("keys1", [P, G, NK], F32R)
            vst[1] = a("values1", [P, NKT, G // 2, 4, DH], F32R)
            qst[1] = a("queries1", [P, 2, G, NQ], F32R)
            wo = a("wo", [P, 2, KC, D], F32R)
            with ExitStack() as staging:
                w_raw = alloc(staging, "w_raw", [P, 4, KC, D])
            probs = a("probs", [P, 4, NK])
            probsT = a("probsT", [P, 2, 3, 2 * NQ], F32R)
            att_tmp = a("att_tmp", [P, NQ])
            att_sum = a("att_sum", [P, NQ])
            attT = a("attT", [P, 2, H // 2, NQ], F32R)
            xres = a("xres", [P, 2, D])
            yT = a("yT", [P, 2, KC, QT], F32R)
            xa = a("xa", [P, 2, D])
            stats = a("stats", [P, 4, 6])
            mean_var = a("mean_var", [P, 4, 2])
            rstd = a("rstd", [P, 4])
            neg_max = a("neg_max", [P, 4])
            row_sum = a("row_sum", [P, 4])
            row_inv = a("row_inv", [P, 4])
            bo_t = a("bo_t", [P, D])

        ffn = st
        xT = alloc(ffn, "xT", [P, 2, KC, N], F32R)
        w_stage = alloc(ffn, "w_stage", [P, 2, HID])
        w1s = alloc(ffn, "w1s", [P, 2, KC, HID], F32R)
        x2_tile = alloc(ffn, "x2_tile", [P, 2, D])
        h_full = alloc(ffn, "h_full", [P, 2, 512])
        b1T = alloc(ffn, "b1T", [P, NE * HT])
        gate_st = alloc(ffn, "gate_st", [P, KC, P], F32R)
        b2_sum = alloc(ffn, "b2_sum", [P, D])
        scaleb = alloc(ffn, "scaleb", [P, 2, NE])
        hs = alloc(ffn, "hs", [P, 2, HT, 512], F32R)
        w2s = alloc(ffn, "w2s", [P, 2, HT, D], F32R)
        acc = alloc(ffn, "acc", [P, TT, D])
        logits = alloc(ffn, "logits", [P, TT, NE])
        logits_tmp = alloc(ffn, "logits_tmp", [P, TT, NE])
        gate_small = alloc(ffn, "gate_small", [P, 6, TT])
        token_gate = alloc(ffn, "token_gate", [P, TT])
        b1_rows = x2_tile[0:NE * HT, 0, 0:P]
        gate_rows = x2_tile[0:NE, 1, :]
        b2_rows = h_full[0:NE, 0, :]
        ones8 = h_full[0:NE, 1, 0:P]

        in_psum = {k: sem(f"{k}_in_psum") for k in "CXKQVTOYSPB"}
        hi_out = {k: sem(f"{k}_hi_out") for k in "CXKQVTYP"}
        lo_out = {k: sem(f"{k}_lo_out") for k in "CXKQVTOYPB"}
        consts_set = sem("consts_set")
        g_loaded, tanh_done = sem("g_loaded"), sem("tanh_done")
        bo_loaded, bo_scaled = sem("bo_loaded"), sem("bo_scaled")
        w_loaded = [sem(f"w_loaded{i}") for i in range(4)]
        w_hi, w_lo = sem("w_hi"), sem("w_lo")
        pool_w_hi, pool_w_lo = sem("pool_w_hi"), sem("pool_w_lo")
        ctx_loaded = [sem(f"ctx_loaded{i}") for i in range(CR)]
        x_loaded = [sem(f"x_loaded{i}") for i in range(2)]
        xres_loaded = [sem(f"xres_loaded{i}") for i in range(2)]
        ln_step, ln_var, ln_rstd, ln_out = sem("ln_step"), sem("ln_var"), sem("ln_rstd"), sem("ln_out")
        xres_biased = sem("xres_biased")
        max_out, exp_out, inv_out = sem("max_out"), sem("exp_out"), sem("inv_out")
        probs_scaled = [sem(f"probs_scaled{i}") for i in range(2)]
        att_hi, att_lo = sem("att_hi"), sem("att_lo")
        x2_stored = [sem(f"x2_stored{i}") for i in range(2)]
        yT_stored = sem("yT_stored")

        xT_loaded = [sem(f"xT_loaded{i}") for i in range(len(CHUNKS))]
        small_loaded, small_set = sem("small_loaded"), sem("small_set")
        scale_loaded = sem("scale_loaded")
        stage_loaded = [sem(f"stage_loaded{i}") for i in range(2)]
        piece_hi, piece_split = sem("piece_hi"), sem("piece_split")
        acc_set = sem("acc_set")
        h_psum, h_act, h_split = sem("h_psum"), sem("h_act"), sem("h_split")
        y_psum, y_added = sem("y_psum"), sem("y_added")
        gate_psum, gate_copied, gate_tr = sem("gate_psum"), sem("gate_copied"), sem("gate_tr")
        gate_step, gate_pow, gate_exp = sem("gate_step"), sem("gate_pow"), sem("gate_exp")
        x2_loaded = [sem(f"x2_loaded{i}") for i in range(2)]
        final_step, out_ready = sem("final_step"), sem("out_ready")
        out_stored = [sem(f"out_stored{i}") for i in range(2)]

        passed = {k: sem(f"{k}_waits_passed") for k in ("sp", "act", "dve", "pool")}

        block = st.enter_context(nc.Block())

        def batches(eng, run):
            run("first", FIRST, 0)
            with eng.Fori(1, B - 1) as b:
                run("middle", MIDDLE, b)
            run("last", LAST, B - 1)

        @block.sync
        def _(sp):
            def load_ctx(b, t):
                if isinstance(b, int) and b == 0:
                    if t >= CR:
                        sp.wait_ge(in_psum["C"], t + 1 - CR)
                else:
                    sp.wait_ge(in_psum["C"], b * NKT + (t + 1 - CR))
                    alone(sp, passed["sp"])
                sp.dma_start(ctx_raw[0:KT, t % CR, :], ctx[b, t * KT:(t + 1) * KT, :]).then_inc(ctx_loaded[t % CR], 16)

            def load_w(i, w):
                sp.dma_start(w_raw[:, i], w.rearrange("(c p) n -> p c n", p=P)).then_inc(w_loaded[i], 16)

            def load_x(b, qt):
                sp.dma_start(xa[0:QT, qt, :], x[b, qt * QT:(qt + 1) * QT, :]).then_inc(x_loaded[qt], 16)

            def load_xres(b, qt):
                sp.dma_start(xres[0:QT, qt, :], x[b, qt * QT:(qt + 1) * QT, :]).then_inc(xres_loaded[qt], 16)

            def store_x2(b, qt):
                sp.wait_ge(lo_out["O"], number(("O", 0, qt), b))
                alone(sp, passed["sp"])
                sp.dma_start(x2_scratch[b, qt * QT:(qt + 1) * QT, :], xres[0:QT, qt, :]).then_inc(x2_stored[qt], 16)

            def store_yT(b, qt):
                sp.wait_ge(lo_out["Y"], number(("Y", 0, qt), b))
                alone(sp, passed["sp"])
                for part in range(2):
                    sp.dma_start(xt_scratch[part, :, :, b, qt * QT:(qt + 1) * QT],
                                 yT[:, part].bitcast(F32)).then_inc(yT_stored, 16)

            def load_xres_next(b):
                for qt in range(2):
                    sp.wait_ge(x2_stored[qt], b * 16)
                    alone(sp, passed["sp"])
                    sp.wait_ge(ln_out, b * 4 + (qt + 1))
                    alone(sp, passed["sp"])
                    load_xres(b, qt)

            sp.dma_start(tanh_g[:, 0:1], g_xattn.partition_broadcast(P)).then_inc(g_loaded, 16)
            sp.dma_start(tanh_g[:, 1:2], g_ffn.partition_broadcast(P)).then_inc(g_loaded, 16)
            load_ctx(0, 0)
            load_ctx(0, 1)
            for qt in range(2):
                load_x(0, qt)
            load_w(0, Wk)
            for t in range(2, NKT):
                load_ctx(0, t)
            load_w(1, Wq)
            load_w(2, Wv)
            load_w(3, Wo)
            sp.dma_start(bo_t[:, :], bo.partition_broadcast(P)).then_inc(bo_loaded, 16)

            def batch(name, plan, b):
                if name != "last":
                    for t in range(CR):
                        load_ctx(b + 1, t)
                if name == "first":
                    sp.wait_ge(w_lo, 2)
                    sp.wait_ge(pool_w_lo, 2)
                    for qt in range(2):
                        load_xres(b, qt)
                else:
                    store_x2(b - 1, 0)
                    store_x2(b - 1, 1)
                    load_xres_next(b)
                for qt in range(2):
                    if name != "first":
                        store_yT(b - 1, qt)
                    if name != "last":
                        if name != "first":
                            sp.wait_ge(in_psum["Y"], number(("Y", -1, qt), b))
                            alone(sp, passed["sp"])
                        sp.wait_ge(in_psum["X"], number(("X", 0, qt), b))
                        alone(sp, passed["sp"])
                        load_x(b + 1, qt)
                        load_ctx(b + 1, CR + qt)
                if name != "last":
                    for t in range(CR + 2, NKT):
                        load_ctx(b + 1, t)

            batches(sp, batch)

            def load_piece(e, which, j, n):
                if not (isinstance(n, int) and n < 2):
                    sp.wait_ge(piece_split, n - 1)
                    alone(sp, passed["sp"])
                if which == 1:
                    src = w1[e, j * P:(j + 1) * P, :]
                    dst = w_stage[:, j % 2, :]
                else:
                    src = w2[e, 2 * j * P:(2 * j + 2) * P, :].rearrange("(c p) n -> p c n", p=P)
                    dst = w_stage[:, j % 2, :].rearrange("p (c n) -> p c n", c=2)
                sp.dma_start(dst, src).then_inc(stage_loaded[j % 2], 16)

            def load_xT(c):
                t0, nt = CHUNKS[c]
                tokens = slice(t0 * P, (t0 + nt) * P)
                for part in range(2):
                    sp.dma_start(xT[:, part, :, tokens].bitcast(F32),
                                 xt_scratch.rearrange("s p c b q -> s p c (b q)")[part, :, :, tokens]
                                 ).then_inc(xT_loaded[c], 16)

            sp.wait_ge(in_psum["V"], number(("V", 0, 1, 5), B - 1))
            sp.wait_ge(in_psum["Q"], number(("Q", 0, 1, 1), B - 1))
            sp.wait_ge(in_psum["P"], number(("P", 0, G - 1), B - 1))
            sp.dma_start(b1_rows, b1.rearrange("e (t p) -> (e t) p", p=P)).then_inc(small_loaded, 16)
            sp.dma_start(gate_rows, gate_w).then_inc(small_loaded, 16)
            sp.dma_start(b2_rows, b2).then_inc(small_loaded, 16)
            sp.dma_start(scaleb[:, 0, :], gate_b.partition_broadcast(P)).then_inc(scale_loaded, 16)
            sp.dma_start(scaleb[:, 1, :], rms_w.partition_broadcast(P)).then_inc(scale_loaded, 16)
            load_piece(0, 1, 0, 0)
            load_piece(0, 1, 1, 1)
            sp.wait_ge(yT_stored, (B - 1) * 64)
            load_xT(0)
            load_piece(0, 1, 2, 2)
            load_piece(0, 1, 3, 3)
            load_xT(1)
            load_piece(0, 2, 0, 4)
            load_piece(0, 2, 1, 5)
            load_xT(2)
            for qt in range(2):
                store_x2(B - 1, qt)
            load_piece(0, 2, 2, 6)
            for qt in range(2):
                store_yT(B - 1, qt)
            load_piece(0, 2, 3, 7)
            sp.wait_ge(yT_stored, B * 64)
            load_xT(3)

            with sp.Fori(1, NE) as e:
                for which in (1, 2):
                    for j in range(4):
                        load_piece(e, which, j, e * 8 + (4 * (which - 1) + j))
            for t in range(TT):
                if t >= 2:
                    sp.wait_ge(out_stored[t % 2], 16 * (t // 2))
                sp.dma_start(x2_tile[:, t % 2, :], x2_scratch.rearrange("b q d -> (b q) d")[t * P:(t + 1) * P, :]
                             ).then_inc(x2_loaded[t % 2], 16)
                if t >= 1:
                    sp.wait_ge(out_ready, t)
                    sp.dma_start(out_rows[(t - 1) * P:t * P, :], x2_tile[:, (t - 1) % 2, :]
                                 ).then_inc(out_stored[(t - 1) % 2], 16)
            sp.wait_ge(out_ready, TT)
            sp.dma_start(out_rows[(TT - 1) * P:, :], x2_tile[:, (TT - 1) % 2, :]).then_inc(out_stored[(TT - 1) % 2], 16)
            for i in range(2):
                sp.wait_ge(out_stored[i], 16 * (TT // 2))

        @block.tensor
        def _(pe):
            def three(bank, parts, first=True, last=True):
                n, total = 0, 3 * len(parts)
                for s, m in parts:
                    for i, j in ((0, 0), (0, 1), (1, 0)):
                        mm = pe.matmul(bank, s[i], m[j], start=first and n == 0, stop=last and n == total - 1)
                        n += 1
                return mm

            def transposes(bank, tile, rows, cols):
                for c in range(KC):
                    t = pe.transpose(bank[:, c * rows:(c + 1) * rows], tile[0:rows, c * cols:(c + 1) * cols],
                                     ident[0:rows, 0:rows])
                return t

            def make(item, b, bank_table):
                kind = item[0]
                if kind in "RMDLAWZ":
                    return
                if kind == "H":
                    return ffn_in_tile(0, 0, item[2])
                n = number(item, b)
                if kind in BANKED:
                    i, before = bank_table[item]
                    bank = ps[i]
                    if before is not None:
                        pe.wait_ge(lo_out[before[0]], number(before, b))
                db = item[1]
                if kind == "C":
                    t = item[2]
                    pe.wait_ge(ctx_loaded[t % CR], (b + db) * (16 * NKT // CR) + 16 * (t // CR + 1))
                    last = transposes(bank, ctx_raw[:, t % CR, :], KT, P)
                elif kind == "X":
                    pe.wait_ge(ln_out, n_ln(0, b + db, item[2]))
                    last = transposes(bank, xa[:, item[2], :], QT, P)
                elif kind == "Y":
                    pe.wait_ge(ln_out, n_ln(1, b + db, item[2]))
                    last = transposes(bank, xa[:, item[2], :], QT, P)
                elif kind == "K":
                    _, _, g, p, half = item
                    k0, k1 = HALVES[half]
                    pe.wait_ge(lo_out["C"], number(("C", db, (k1 - 1) // KT), b))
                    cols = slice((2 * g + p) * P, (2 * g + p + 1) * P)
                    keys = slice(k0, k1)
                    last = three(bank[:, 0:k1 - k0], [([wk[:, s, c, cols] for s in range(2)],
                                                    [ctxT[:, s, c, keys] for s in range(2)]) for c in range(KC)])
                elif kind == "Q":
                    _, _, g, p = item
                    pe.wait_ge(lo_out["X"], number(("X", db, 1), b))
                    cols = slice((2 * g + p) * P, (2 * g + p + 1) * P)
                    last = three(bank[:, 0:NQ], [([wq[:, s, c, cols] for s in range(2)],
                                                  [xnT[:, s, c, :] for s in range(2)]) for c in range(KC)])
                elif kind == "V":
                    _, _, g, t = item
                    pe.wait_ge(lo_out["C"], number(("C", db, t), b))
                    keys = slice(t * KT, (t + 1) * KT)
                    cols = slice(g * G * DH, (g + 1) * G * DH)
                    last = three(bank[0:KT, 0:G * DH], [([ctxT[:, s, c, keys] for s in range(2)],
                                                         [wv[:, s, c, cols] for s in range(2)]) for c in range(KC)])
                elif kind == "S":
                    _, _, h, qt = item[:4]
                    g, hh = h // G, h % G
                    pe.wait_ge(lo_out["K"], number(("K", db, g, hh // 2, 1), b))
                    pe.wait_ge(lo_out["Q"], number(("Q", db, g, hh // 2), b))
                    if not (isinstance(b, int) and n <= 2):
                        pe.wait_ge(exp_out, n - 2)
                    rows = slice(qt * QT, (qt + 1) * QT)
                    for third in range(3):
                        for s in range(2):
                            last = pe.matmul(ps_scores[qt][0:QT, third, 0:SK], qst[g][:, s, hh, rows],
                                             kst[g][:, hh, third * SK:(third + 1) * SK], start=s == 0, stop=s == 1)
                elif kind == "T":
                    _, _, h, k = item
                    if k == 0:
                        for qt in range(2):
                            pe.wait_ge(probs_scaled[qt], (b + db) * H + (h + 1))
                    for kt in range(2 * k, 2 * k + 2):
                        for qt in range(2):
                            at = (kt % 2) * NQ + qt * QT
                            last = pe.transpose(bank[0:KT, at:at + QT],
                                                probs[0:QT, (h % 2) * 2 + qt, kt * KT:(kt + 1) * KT],
                                                ident[0:QT, 0:QT])
                elif kind == "P":
                    h = item[2]
                    g, hh = h // G, h % G
                    odd = h % 2
                    pe.wait_ge(lo_out["V"], number(("V", db, g, NKT - 1), b))
                    for kt in range(NKT):
                        if kt % 2 == 0:
                            pe.wait_ge(lo_out["T"], number(("T", 0, h, kt // 2), b))
                        v = vst[g][0:KT, kt, hh // 2, 2 * odd:2 * odd + 2, :].rearrange("p s d -> p (s d)")
                        for s in range(2):
                            last = pe.matmul(bank[:, 0:NQ], v,
                                             probsT[0:KT, s, kt // 2, (kt % 2) * NQ:(kt % 2 + 1) * NQ],
                                             start=kt == 0 and s == 0, stop=kt == NKT - 1 and s == 1)
                elif kind == "O":
                    qt = item[2]
                    pe.wait_ge(att_lo, (b + db + 1) * (H // 2))
                    rows = slice(qt * QT, (qt + 1) * QT)
                    last = three(bank[0:QT, :], [([attT[:, s, c, rows] for s in range(2)],
                                                  [wo[:, s, c, :] for s in range(2)]) for c in range(KC)])
                elif kind == "B":
                    pe.wait_ge(small_loaded, 48)
                    if item[2] == 0:
                        last = pe.transpose(bank[:, 0:NE * HT], b1_rows, ident[0:NE * HT, 0:NE * HT])
                    elif item[2] == 1:
                        for c in range(KC):
                            last = pe.transpose(bank[:, c * NE:(c + 1) * NE], gate_rows[:, c * P:(c + 1) * P],
                                                ident[0:NE, 0:NE])
                    else:
                        pe.wait_ge(small_set, 1)
                        last = pe.matmul(bank[:, :], ones8, b2_rows, start=True, stop=True)
                last.then_inc(in_psum[kind], 1)

            hb = [ps_scores[i // 2][:, 2 * (i % 2):2 * (i % 2) + 2, :].rearrange("p a n -> p (a n)") for i in range(4)]

            def ffn_in_tile(e, c, t):
                t0, nt = CHUNKS[c]
                if t == 0:
                    pe.wait_ge(piece_split, e * 8 + 4)
                    pe.wait_ge(xT_loaded[c], 32)
                    pe.wait_ge(exp_out, 16 * B)
                k = c * HT + t
                if k >= 4:
                    pe.wait_ge(h_act, e * (4 * HT) + (k - 3))
                three(hb[t % 4][:, 0:nt * P],
                      [([w1s[:, s, kc, t * P:(t + 1) * P] for s in range(2)],
                        [xT[:, s, kc, t0 * P:(t0 + nt) * P] for s in range(2)]) for kc in range(KC)]
                      ).then_inc(h_psum, 1)

            pe.wait_ge(consts_set, 3)
            waited_w = set()
            for item in HEAD_PLAN:
                w = {"K": 0, "Q": 1, "V": 2}.get(item[0])
                if w is not None and w not in waited_w:
                    waited_w.add(w)
                    if w < 2:
                        pe.wait_ge(w_lo, w + 1)
                    else:
                        pe.wait_ge(pool_w_lo, 1)
                make(item, 0, bank_of["head"])
            pe.wait_ge(pool_w_lo, 2)

            def batch(name, plan, b):
                for item in plan:
                    make(item, b, bank_of[name])

            batches(pe, batch)
            for item in TAIL_PLAN:
                make(item, B - 1, bank_of["tail"])

            def ffn_in(e, c):
                for t in range(HT):
                    ffn_in_tile(e, c, t)

            def ffn_out(e, c, ts=None):
                t0, nt = CHUNKS[c]
                for t in ts or range(nt):
                    k = t0 + t
                    if k >= 2:
                        pe.wait_ge(y_added, e * TT + (k - 1))
                    for ht in range(HT):
                        if t == 0:
                            pe.wait_ge(h_split, e * (4 * HT) + (c * HT + ht + 1))
                        if k == 0 and ht % 2 == 0:
                            pe.wait_ge(piece_split, e * 8 + (5 + ht // 2))
                        mm = three(ps[k % 2][:, :], [([hs[:, s, ht, t * P:(t + 1) * P] for s in range(2)],
                                                      [w2s[:, s, ht, :] for s in range(2)])],
                                   first=ht == 0, last=ht == HT - 1)
                    mm.then_inc(y_psum, 1)

            with pe.Fori(0, NE - 1) as e:
                for c in range(len(CHUNKS)):
                    if c:
                        ffn_in(e, c)
                    ffn_out(e, c)
                ffn_in(e + 1, 0)
            e = NE - 1
            pe.wait_ge(lo_out["B"], 3)
            for c, (t0, nt) in enumerate(CHUNKS):
                pe.wait_ge(h_act, e * 4 * HT + 5 + c)
                for kc in range(KC):
                    for s in range(2):
                        mm = pe.matmul(hb[c][:, 0:nt * P], gate_st[:, kc, :], xT[:, s, kc, t0 * P:(t0 + nt) * P],
                                       start=kc == 0 and s == 0, stop=kc == KC - 1 and s == 1)
                mm.then_inc(gate_psum, 1)
            for half in range(2):
                ffn_out(e, 0, (2 * half, 2 * half + 1))
                for c in (2 * half, 2 * half + 1):
                    t0, nt = CHUNKS[c]
                    pe.wait_ge(gate_copied, c + 1)
                    for t in range(nt):
                        tr = pe.transpose(ps[2][:, (t0 + t) * 16:(t0 + t + 1) * 16],
                                          h_full[0:16, c % 2, t * P:(t + 1) * P], ident[0:16, 0:16])
                    tr.then_inc(gate_tr, 1)
            for c in range(1, len(CHUNKS)):
                ffn_in(e, c)
                ffn_out(e, c)

        @block.vector
        def _(dve):
            def split_w(i, w):
                dve.wait_ge(w_hi, i + 1)
                dve.tensor_tensor(w[:, 1], w_raw[:, i], w[:, 0].bitcast(F32), ALU.subtract).then_inc(w_lo, 1)

            def lnorm_stats(which, b, src, slot):
                n = n_ln(which, b, slot % 2)
                dve.bn_stats(stats[0:QT, slot, :], src).then_inc(ln_step, 1)
                dve.wait_ge(ln_step, n * 2 - 1)
                alone(dve, passed["dve"])
                dve.bn_aggr(mean_var[0:QT, slot, :], stats[0:QT, slot, :]).then_inc(ln_step, 1)
                dve.wait_ge(ln_step, n * 2)
                dve.tensor_scalar(rstd[0:QT, slot:slot + 1], mean_var[0:QT, slot, 1:2], LN_EPS, None,
                                  ALU.add).then_inc(ln_var, 1)

            def lnorm_apply(which, b, src, dst, slot):
                dve.wait_ge(ln_rstd, n_ln(which, b, slot % 2))
                dve.tensor_scalar(dst, src, mean_var[0:QT, slot, 0:1], rstd[0:QT, slot:slot + 1],
                                  ALU.subtract, ALU.mult).then_inc(ln_out, 1)

            def sub(out, a_, b_):
                return dve.tensor_tensor(out, a_, b_.bitcast(F32), ALU.subtract)

            def drain(item, b, bank_table):
                kind, db = item[0], item[1]
                if kind in "RMDPSO":
                    return special(item, b, bank_table)
                if kind == "L":
                    which, qt = item[2:]
                    if which == 0:
                        dve.wait_ge(x_loaded[qt], (b + db) * 16 + 16)
                        return lnorm_stats(0, b + db, xa[0:QT, qt, :], qt)
                    dve.wait_ge(lo_out["O"], number(("O", db, qt), b))
                    return lnorm_stats(1, b + db, xres[0:QT, qt, :], 2 + qt)
                if kind == "A":
                    which, qt = item[2:]
                    src = xres if which else xa
                    return lnorm_apply(which, b + db, src[0:QT, qt, :], xa[0:QT, qt, :], 2 * which + qt)
                if kind == "W":
                    return split_piece(0, 1, item[2], item[2])
                if kind == "Z":
                    return
                if kind == "H":
                    t = item[2]
                    hidden_tile(0, 0, t)
                    if 2 <= t < 6:
                        split_piece(0, 2, t - 2, t + 2)
                    return
                if kind == "B":
                    bank = ps[bank_table[item][0]]
                    dve.wait_ge(in_psum["B"], item[2] + 1)
                    if item[2] == 0:
                        last = dve.tensor_copy(b1T[:, :], bank[:, 0:NE * HT])
                    elif item[2] == 1:
                        dve.wait_ge(small_set, 2)
                        gw = bank[:, 0:KC * NE].rearrange("p (c n) -> p c n", c=KC)
                        dve.tensor_copy(gate_st[:, :, 0:NE], gw).then_inc(gate_step, 1)
                        dve.wait_ge(gate_step, 1)
                        last = sub(gate_st[:, :, NE:2 * NE], gw, gate_st[:, :, 0:NE])
                    else:
                        last = dve.tensor_copy(b2_sum[:, :], bank[:, :])
                    last.then_inc(lo_out["B"], 1)
                    return
                bank = ps[bank_table[item][0]]
                n = number(item, b)
                dve.wait_ge(hi_out[kind], n)
                if kind == "C":
                    t = item[2]
                    cols = slice(t * KT, (t + 1) * KT)
                    last = sub(ctxT[:, 1, :, cols], bank[:, 0:KC * KT].rearrange("p (c k) -> p c k", c=KC),
                               ctxT[:, 0, :, cols])
                elif kind == "X":
                    cols = slice(item[2] * QT, (item[2] + 1) * QT)
                    last = sub(xnT[:, 1, :, cols], bank[:, 0:KC * QT].rearrange("p (c k) -> p c k", c=KC),
                               xnT[:, 0, :, cols])
                elif kind == "Y":
                    last = sub(yT[:, 1], bank[:, 0:KC * QT].rearrange("p (c k) -> p c k", c=KC), yT[:, 0])
                elif kind == "K":
                    _, _, g, p, half = item
                    keys = slice(*HALVES[half])
                    n = keys.stop - keys.start
                    sub(kst[g][64:128, 2 * p, keys], bank[0:64, 0:n], kst[g][0:64, 2 * p, keys])
                    last = sub(kst[g][0:64, 2 * p + 1, keys], bank[64:128, 0:n], kst[g][64:128, 2 * p + 1, keys])
                elif kind == "Q":
                    _, _, g, p = item
                    for odd in range(2):
                        src = slice(64 * odd, 64 * odd + 64)
                        for to in range(2):
                            last = dve.scalar_tensor_tensor(
                                qst[g][64 * to:64 * to + 64, 1, 2 * p + odd, :], bank[src, 0:NQ], DH ** -0.5,
                                qst[g][src, 0, 2 * p + odd, :].bitcast(F32), ALU.mult, ALU.subtract)
                elif kind == "V":
                    _, _, g, t = item
                    last = sub(vst[g][0:KT, t, :, 1:3, :],
                               bank[0:KT, 0:G * DH].rearrange("p (a s d) -> p a s d", a=2, s=2),
                               vst[g][0:KT, t, :, 0::3, :])
                elif kind == "T":
                    k = item[3]
                    last = sub(probsT[0:KT, 1, k, :], bank[0:KT, 0:2 * NQ], probsT[0:KT, 0, k, :])
                last.then_inc(lo_out[kind], 1)

            def special(item, b, bank_table):
                kind, db = item[0], item[1]
                if kind == "S":
                    _, _, h, qt = item[:4]
                    i = (h % 2) * 2 + qt
                    dve.wait_ge(in_psum["S"], number(item, b))
                    dve.tensor_reduce(neg_max[0:QT, i:i + 1], ps_scores[qt][0:QT, 0:3, 0:SK], AX.XY, ALU.max,
                                      negate=True).then_inc(max_out, 1)
                elif kind == "R":
                    _, _, h, qt = item[:4]
                    i = (h % 2) * 2 + qt
                    dve.wait_ge(exp_out, number(item, b))
                    dve.reciprocal(row_inv[0:QT, i:i + 1], row_sum[0:QT, i:i + 1]).then_inc(inv_out, 1)
                elif kind == "M":
                    _, _, h, qt = item
                    i = (h % 2) * 2 + qt
                    if SCALER[qt] == "dve":
                        dve.wait_ge(inv_out, number(item, b))
                        dve.tensor_scalar(probs[0:QT, i, :], probs[0:QT, i, :], row_inv[0:QT, i:i + 1], None,
                                          ALU.mult).then_inc(probs_scaled[qt], 1)
                elif kind == "D":
                    h = item[2]
                    n = number(item, b)
                    bank = ps[bank_table[("P", db, h)][0]] if ("P", db, h) in bank_table else ps[RING - 1]
                    rows = slice(64 * (h % 2), 64 * (h % 2) + 64)
                    dve.wait_ge(hi_out["P"], n)
                    if h % 2 == 0 and not (isinstance(b, int) and n == 1):
                        dve.wait_ge(att_lo, (b + db) * (H // 2) + h // 2)
                    last = dve.tensor_tensor(att_sum[rows, :], bank[rows, 0:NQ], att_tmp[rows, :], ALU.add)
                    last.then_inc(lo_out["P"], 1)
                elif kind == "O":
                    qt = item[2]
                    n = number(item, b)
                    dve.wait_ge(in_psum["O"], n)
                    dve.wait_ge(xres_biased, n)
                    dve.scalar_tensor_tensor(xres[0:QT, qt, :], ps[bank_table[item][0]][0:QT, :], tanh_g[0:QT, 0:1],
                                             xres[0:QT, qt, :], ALU.mult, ALU.add).then_inc(lo_out["O"], 1)

            dve.wait_ge(consts_set, 3)
            todo = [wk, wq]
            k = 0
            for item in HEAD_PLAN:
                drain(item, 0, bank_of["head"])
                if item in SPLIT_AT:
                    split_w(k, todo[k])
                    k += 1
            dve.wait_ge(bo_loaded, 16)
            dve.wait_ge(tanh_done, 1)
            dve.tensor_scalar(bo_t[:, :], bo_t[:, :], tanh_g[:, 0:1], None, ALU.mult).then_inc(bo_scaled, 1)

            def split_piece(e, which, j, n):
                dve.wait_ge(stage_loaded[j % 2], e * 64 + (16 * (j // 2 + 1) + 32 * (which - 1)))
                if which == 1:
                    dst = [w1s[:, s, j, :] for s in range(2)]
                else:
                    dst = [w2s[:, s, 2 * j:2 * j + 2, :].rearrange("p c n -> p (c n)") for s in range(2)]
                dve.tensor_copy(dst[0], w_stage[:, j % 2, :]).then_inc(piece_hi, 1)
                dve.wait_ge(piece_hi, n + 1)
                sub(dst[1], w_stage[:, j % 2, :], dst[0]).then_inc(piece_split, 1)

            def hidden_tile(e, c, t):
                nt = CHUNKS[c][1]
                dve.wait_ge(h_act, e * (4 * HT) + (c * HT + t + 1))
                sub(hs[:, 1, t, 0:nt * P], h_full[:, t % 2, 0:nt * P], hs[:, 0, t, 0:nt * P]).then_inc(h_split, 1)

            def batch(name, plan, b):
                for item in plan:
                    drain(item, b, bank_of[name])

            batches(dve, batch)
            batch("tail", TAIL_PLAN, B - 1)
            def hidden(e, c):
                for t in range(HT):
                    hidden_tile(e, c, t)
                    if c == 0 and t % 2 == 0:
                        split_piece(e, 2, t // 2, e * 8 + (4 + t // 2))

            def add_up(e, k):
                dve.wait_ge(y_psum, e * TT + (k + 1))
                for c, (t0, _) in enumerate(CHUNKS):
                    if k == t0:
                        dve.wait_ge(acc_set, c + 1)
                dve.tensor_tensor(acc[:, k, :], ps[k % 2][:, :], acc[:, k, :], ALU.add).then_inc(y_added, 1)

            with dve.Fori(0, NE - 1) as e:
                for c, (t0, nt) in enumerate(CHUNKS):
                    if c:
                        hidden(e, c)
                    for t in range(nt):
                        if c == 3:
                            if t == 0:
                                dve.wait_ge(h_psum, e * (4 * HT) + 4 * HT)
                                split_piece(e + 1, 1, 0, e * 8 + 8)
                                split_piece(e + 1, 1, 1, e * 8 + 9)
                            elif t == 1:
                                split_piece(e + 1, 1, 2, e * 8 + 10)
                                split_piece(e + 1, 1, 3, e * 8 + 11)
                        add_up(e, t0 + t)
                hidden(e + 1, 0)

            e = NE - 1
            step = [1]

            def chain(ins):
                ins.then_inc(gate_step, 1)
                step[0] += 1
                dve.wait_ge(gate_step, step[0])

            for k in range(CHUNKS[0][1]):
                add_up(e, k)
            dve.wait_ge(gate_tr, 4)
            dve.wait_ge(scale_loaded, 32)
            pair = ps[2][:, 0:TT * 16].rearrange("p (t n) -> p t n", t=TT)
            chain(dve.tensor_copy(logits_tmp[:, :, :], pair[:, :, NE:2 * NE]))
            chain(dve.tensor_tensor(logits[:, :, :], pair[:, :, 0:NE], logits_tmp[:, :, :], ALU.add))
            chain(dve.tensor_tensor(logits[:, :, :], logits[:, :, :],
                                    scaleb[:, 0:1, :].to_broadcast([P, TT, NE]), ALU.add))
            chain(dve.tensor_tensor(logits_tmp[:, :, :], logits[:, :, :], logits[:, :, :], ALU.mult))
            chain(dve.tensor_reduce(gate_small[:, 0, :], logits_tmp[:, :, :], AX.X, ALU.add))
            chain(dve.tensor_scalar(gate_small[:, 1, :], gate_small[:, 0, :], 1.0 / NE, RMS_EPS, ALU.mult, ALU.add))
            dve.wait_ge(gate_pow, 1)
            chain(dve.tensor_tensor(logits[:, :, :], logits[:, :, :],
                                    gate_small[:, 2, :].unsqueeze(2).to_broadcast([P, TT, NE]), ALU.mult))
            chain(dve.tensor_tensor(logits[:, :, :], logits[:, :, :],
                                    scaleb[:, 1:2, :].to_broadcast([P, TT, NE]), ALU.mult))
            chain(dve.tensor_reduce(gate_small[:, 3, :], logits[:, :, :], AX.X, ALU.max))
            chain(dve.tensor_tensor(logits[:, :, :], logits[:, :, :],
                                    gate_small[:, 3, :].unsqueeze(2).to_broadcast([P, TT, NE]), ALU.subtract))
            hidden(e, 1)
            dve.wait_ge(gate_exp, 1)
            chain(dve.tensor_reduce(gate_small[:, 0, :], logits_tmp[:, :, :], AX.X, ALU.add))
            chain(dve.reciprocal(gate_small[:, 1, :], gate_small[:, 0, :]))
            chain(dve.tensor_scalar(gate_small[:, 3, :], gate_small[:, 1, :], NORM_EPS, None, ALU.add))
            chain(dve.reciprocal(gate_small[:, 4, :], gate_small[:, 3, :]))
            chain(dve.tensor_tensor(gate_small[:, 5, :], gate_small[:, 1, :], gate_small[:, 4, :], ALU.mult))
            chain(dve.tensor_scalar(token_gate[:, :], gate_small[:, 5, :], tanh_g[:, 1:2], None, ALU.mult))

            def result(k):
                dve.wait_ge(y_added, e * TT + k + 1)
                dve.wait_ge(x2_loaded[k % 2], 16 * (k // 2 + 1))
                dve.scalar_tensor_tensor(x2_tile[:, k % 2, :], acc[:, k, :], token_gate[:, k:k + 1],
                                         x2_tile[:, k % 2, :], ALU.mult, ALU.add).then_inc(out_ready, 1)

            done = 0
            for c, (t0, nt) in enumerate(CHUNKS[1:], 1):
                if c >= 2:
                    for t in range(HT):
                        hidden_tile(e, c, t)
                        if t % 2 and done < t0:
                            result(done)
                            done += 1
                for k in range(t0, t0 + nt):
                    add_up(e, k)
                    result(done)
                    done += 1

        @block.scalar
        def _(act):
            def copy(dst, src, scale=1.0):
                return act.activation(dst, src, ACT.Copy, scale=scale)

            def hi(item, b, bank_table):
                kind, db = item[0], item[1]
                if kind == "M" and SCALER[item[3]] == "act":
                    _, _, h, qt = item
                    i = (h % 2) * 2 + qt
                    act.wait_ge(inv_out, number(item, b))
                    alone(act, passed["act"])
                    copy(probs[0:QT, i, :], probs[0:QT, i, :],
                         scale=row_inv[0:QT, i:i + 1]).then_inc(probs_scaled[qt], 1)
                    return
                if kind in "RMDLAWOZB":
                    return
                if kind == "H":
                    return gelu_tile(0, 0, item[2])
                n = number(item, b)
                if kind == "S":
                    _, _, h, qt = item[:4]
                    i = (h % 2) * 2 + qt
                    act.wait_ge(max_out, n)
                    if not (isinstance(b, int) and n <= 4):
                        act.wait_ge(in_psum["T"], number(("T", db, h, 2), b) - 6)
                        act.wait_ge(inv_out, n - 4)
                    act.activation(probs[0:QT, i, :].rearrange("p (a k) -> p a k", a=3),
                                   ps_scores[qt][0:QT, 0:3, 0:SK], ACT.Exp, bias=neg_max[0:QT, i:i + 1],
                                   accum_out=row_sum[0:QT, i:i + 1]).then_inc(exp_out, 1)
                    return
                if kind == "P":
                    here, there = (0, 64) if item[2] % 2 == 0 else (64, 0)
                    act.wait_ge(in_psum["P"], n)
                    if not (isinstance(b, int) and n <= 2):
                        act.wait_ge(lo_out["P"], n - 2)
                    copy(att_tmp[here:here + 64, :],
                         ps[bank_table[item][0]][there:there + 64, 0:NQ]).then_inc(hi_out["P"], 1)
                    return
                bank = ps[bank_table[item][0]]
                act.wait_ge(in_psum[kind], n)
                if kind == "C":
                    t = item[2]
                    if db:
                        act.wait_ge(in_psum["K"], number(("K", 0, 1, 1, 1), b))
                        act.wait_ge(in_psum["V"], number(("V", 0, 1, t), b))
                    last = copy(ctxT[:, 0, :, t * KT:(t + 1) * KT],
                                bank[:, 0:KC * KT].rearrange("p (c k) -> p c k", c=KC))
                elif kind == "X":
                    if db:
                        act.wait_ge(in_psum["Q"], number(("Q", 0, 1, 1), b))
                    cols = slice(item[2] * QT, (item[2] + 1) * QT)
                    last = copy(xnT[:, 0, :, cols], bank[:, 0:KC * QT].rearrange("p (c k) -> p c k", c=KC))
                elif kind == "Y":
                    if item[2] == 1:
                        act.wait_ge(yT_stored, (b + db) * 64 + 32)
                    elif not (isinstance(b, int) and b + db == 0):
                        act.wait_ge(yT_stored, (b + db) * 64)
                    last = copy(yT[:, 0], bank[:, 0:KC * QT].rearrange("p (c k) -> p c k", c=KC))
                elif kind == "K":
                    _, _, g, p, half = item
                    keys = slice(*HALVES[half])
                    n = keys.stop - keys.start
                    copy(kst[g][0:64, 2 * p, keys], bank[0:64, 0:n])
                    last = copy(kst[g][64:128, 2 * p + 1, keys], bank[64:128, 0:n])
                elif kind == "Q":
                    _, _, g, p = item
                    for odd in range(2):
                        for to in range(2):
                            last = copy(qst[g][64 * to:64 * to + 64, 0, 2 * p + odd, :],
                                        bank[64 * odd:64 * odd + 64, 0:NQ], scale=DH ** -0.5)
                elif kind == "V":
                    _, _, g, t = item
                    last = copy(vst[g][0:KT, t, :, 0::3, :],
                                bank[0:KT, 0:G * DH].rearrange("p (a s d) -> p a s d", a=2, s=2))
                elif kind == "T":
                    k = item[3]
                    last = copy(probsT[0:KT, 0, k, :], bank[0:KT, 0:2 * NQ])
                last.then_inc(hi_out[kind], 1)

            hb = [ps_scores[i // 2][:, 2 * (i % 2):2 * (i % 2) + 2, :].rearrange("p a n -> p (a n)") for i in range(4)]

            def gelu_tile(e, c, t):
                nt = CHUNKS[c][1]
                k = c * HT + t
                act.wait_ge(h_psum, e * (4 * HT) + (k + 1))
                if not (isinstance(e, int) and e == 0 and k < 2):
                    act.wait_ge(h_split, e * (4 * HT) + (k - 1))
                alone(act, passed["act"])
                bias = b1T[:, bass.ds(e * HT + t, 1)]
                act.activation(h_full[:, t % 2, 0:nt * P], hb[t % 4][:, 0:nt * P], ACT.Gelu, bias=bias)
                act.activation(hs[:, 0, t, 0:nt * P], hb[t % 4][:, 0:nt * P], ACT.Gelu, bias=bias).then_inc(h_act, 1)

            def gelu(e, c):
                for t in range(HT):
                    gelu_tile(e, c, t)

            act.wait_ge(g_loaded, 32)
            act.activation(tanh_g[:, :], tanh_g[:, :], ACT.Tanh).then_inc(tanh_done, 1)
            order = {SPLIT_AT[0]: (0, wk), SPLIT_AT[1]: (1, wq)}
            for item in HEAD_PLAN:
                hi(item, 0, bank_of["head"])
                if item in order:
                    i, w = order[item]
                    act.wait_ge(w_loaded[i], 16)
                    copy(w[:, 0], w_raw[:, i]).then_inc(w_hi, 1)

            batches(act, lambda name, plan, b: [hi(item, b, bank_of[name]) for item in plan])
            act.wait_ge(lo_out["B"], 1)
            for item in TAIL_PLAN:
                hi(item, B - 1, bank_of["tail"])

            with act.Fori(0, NE - 1) as e:
                for c in range(1, len(CHUNKS)):
                    gelu(e, c)
                gelu(e + 1, 0)
            e = NE - 1
            for c, (t0, nt) in enumerate(CHUNKS):
                act.wait_ge(gate_psum, c + 1)
                act.wait_ge(h_split, e * 4 * HT + HT)
                if c >= 2:
                    act.wait_ge(gate_tr, c - 1)
                copy(h_full[0:16, c % 2, 0:nt * P], hb[c][0:16, 0:nt * P]).then_inc(gate_copied, 1)
            act.wait_ge(gate_tr, 4)
            gelu(e, 1)
            act.wait_ge(gate_step, 11)
            act.activation(logits_tmp[:, :, :], logits[:, :, :], ACT.Exp, scale=1.0 / TEMPERATURE).then_inc(gate_exp, 1)
            for c in range(2, len(CHUNKS)):
                gelu(e, c)

        @block.gpsimd
        def _(pool):
            pool.memset(ident[:, :], 0.0).then_inc(consts_set, 1)
            pool.wait_ge(consts_set, 1)
            pool.affine_select(out=ident[:, :], in_=ident[:, :], compare_op=ALU.not_equal, fill=1.0, base=0,
                               pattern=[[-1, P]], channel_multiplier=1).then_inc(consts_set, 1)
            pool.memset(minus_half[:, :], -0.5).then_inc(consts_set, 1)
            pool.wait_ge(consts_set, 3)

            def inv_sqrt(which, b, slot):
                pool.wait_ge(ln_var, n_ln(which, b, slot % 2))
                pool.tensor_tensor(rstd[0:QT, slot:slot + 1], rstd[0:QT, slot:slot + 1], minus_half[0:QT, 0:1],
                                   ALU.pow).then_inc(ln_rstd, 1)

            def handle(item, b):
                kind, db = item[0], item[1]
                if kind == "M" and SCALER[item[3]] == "pool":
                    _, _, h, qt = item[:4]
                    i = (h % 2) * 2 + qt
                    pool.wait_ge(inv_out, number(item, b))
                    alone(pool, passed["pool"])
                    pool.tensor_scalar(probs[0:QT, i, :], probs[0:QT, i, :], row_inv[0:QT, i:i + 1], None,
                                       ALU.mult).then_inc(probs_scaled[qt], 1)
                elif kind == "D" and item[2] % 2:
                    pair = item[2] // 2
                    n = (b + db) * (H // 2) + (pair + 1)
                    pool.wait_ge(lo_out["P"], number(item, b))
                    if pair == 0 and not (isinstance(b, int) and b == 0):
                        pool.wait_ge(in_psum["O"], (b + db) * 2)
                    alone(pool, passed["pool"])
                    pool.tensor_copy(attT[:, 0, pair, :], att_sum[:, :]).then_inc(att_hi, 1)
                    pool.wait_ge(att_hi, n)
                    pool.tensor_tensor(attT[:, 1, pair, :], att_sum[:, :], attT[:, 0, pair, :].bitcast(F32),
                                       ALU.subtract).then_inc(att_lo, 1)
                    if pair == 1:
                        bias_x(b)
                elif kind == "Z":
                    pool.wait_ge(in_psum["V"], number(("V", 0, 1, 5), B - 1))
                    pool.wait_ge(in_psum["Q"], number(("Q", 0, 1, 1), B - 1))
                    pool.wait_ge(in_psum["P"], number(("P", 0, G - 1), B - 1))
                    pool.memset(ones8, 1.0).then_inc(small_set, 1)
                    pool.memset(gate_st[:, :, :].bitcast(F32), 0.0).then_inc(small_set, 1)
                elif kind == "L":
                    which, qt = item[2:]
                    inv_sqrt(which, b + db, 2 * which + qt)

            def bias_x(b):
                pool.wait_ge(bo_scaled, 1)
                for qt in range(2):
                    pool.wait_ge(xres_loaded[qt], b * 16 + 16)
                    pool.tensor_tensor(xres[0:QT, qt, :], xres[0:QT, qt, :], bo_t[0:QT, :],
                                       ALU.add).then_inc(xres_biased, 1)

            for item in HEAD_PLAN:
                handle(item, 0)
                if item == ("L", 0, 0, 1):
                    for i, w in ((2, wv), (3, wo)):
                        pool.wait_ge(w_loaded[i], 16)
                        pool.tensor_copy(w[:, 0], w_raw[:, i]).then_inc(pool_w_hi, 1)
                        pool.wait_ge(pool_w_hi, i - 1)
                        pool.tensor_tensor(w[:, 1], w_raw[:, i], w[:, 0].bitcast(F32), ALU.subtract).then_inc(pool_w_lo, 1)

            def batch(name, plan, b):
                for item in plan:
                    handle(item, b)

            batches(pool, batch)
            for item in TAIL_PLAN:
                handle(item, B - 1)

            pool.wait_ge(lo_out["B"], 3)
            for qt in range(2):
                pool.wait_ge(x2_stored[qt], B * 16)
            pool.wait_ge(yT_stored, B * 64)
            for t0, nt in CHUNKS:
                pool.tensor_copy(acc[:, t0:t0 + nt, :],
                                 b2_sum[:, :].unsqueeze(1).to_broadcast([P, nt, D])).then_inc(acc_set, 1)
            pool.wait_ge(gate_step, 7)
            pool.tensor_tensor(gate_small[:, 2, :], gate_small[:, 1, :], minus_half[:, 0:TT],
                               ALU.pow).then_inc(gate_pow, 1)


def n_ln(which, b, qt):
    if which == 0:
        if isinstance(b, int) and b == 0:
            return qt + 1
        return b * 4 + (qt - 1)
    if isinstance(b, int) and b == B - 1:
        return 4 * B - 2 + qt + 1
    return b * 4 + (qt + 5)


_INS = ['x', 'ctx_1024', 'g_xattn', 'g_ffn', 'L0_xattn_Wq', 'L0_xattn_Wk', 'L0_xattn_Wv', 'L0_xattn_Wo',
        'L0_xattn_bo', 'L0_ffn_gate_w', 'L0_ffn_gate_b', 'L0_ffn_rms_w', 'L0_ffn_w1', 'L0_ffn_b1', 'L0_ffn_w2',
        'L0_ffn_b2']


def kernel(**inputs):
    import numpy as _np
    import concourse.bacc as _bacc
    from concourse import mybir as _mybir
    from concourse.bass_utils import run_bass_kernel_spmd as _run

    nc = _bacc.Bacc("TRN2", target_bir_lowering=False, num_devices=1)
    arrays, args = {}, []
    for name in _INS:
        a = _np.ascontiguousarray(inputs[name])
        arrays[f"in_{name}"] = a
        args.append(nc.dram_tensor(f"in_{name}", a.shape, _mybir.dt.from_np(a.dtype), kind="ExternalInput").ap())
    args.append(nc.dram_tensor("out_0", (B, NQ, D), F32, kind="ExternalOutput").ap())
    args.append(nc.dram_tensor("x2_scratch", (B, NQ, D), F32, kind="Internal").ap())
    args.append(nc.dram_tensor("xt_scratch", (2, P, KC, B, NQ), F32, kind="Internal").ap())
    flamingo_kernel(nc, *args)
    r = _run(nc, [arrays], core_ids=[0])
    return r.results[0]["out_0"]
```
